# Optimizing a Trainium2 kernel written in Bass

```python
import numpy as np
import jax
import jax.numpy as jnp

def _softmax(x, axis=-1):
    return jax.nn.softmax(x, axis=axis)

def _gelu(x):
    return jax.nn.gelu(x, approximate=True)

def _silu(x):
    return jax.nn.silu(x)

def _sigmoid(x):
    return jax.nn.sigmoid(x)

def _layernorm(x, axis=-1, eps=1e-05):
    m = jnp.mean(x, axis=axis, keepdims=True)
    v = jnp.var(x, axis=axis, keepdims=True)
    return (x - m) / jnp.sqrt(v + eps)

def _scatter_add(tgt, idx, src, axis=0):
    return tgt.at[idx].add(src)

def _segment_sum(src, seg, n):
    return jax.ops.segment_sum(src, seg, n)
kernel_name = 'mk_perceiver_d1_seqx_r2_55089e'

def setup_inputs(seed: int=0):
    np.random.seed(seed)
    _w = jnp.asarray

    def _rec_inputs():
        import jax
        import jax.numpy as jnp
        _rk = jax.random.key(seed)
        x = 7.22e-05 + 1 * jax.random.normal(jax.random.fold_in(_rk, 1), (1, 512, 512), jnp.float32)
        _lenS = 512 - jax.random.randint(jax.random.fold_in(_rk, 7), (1,), 0, max(1, 512 // 4) + 1, jnp.int32)
        _lenS2 = 8192 - jax.random.randint(jax.random.fold_in(_rk, 8), (1,), 0, max(1, 8192 // 4) + 1, jnp.int32)
        _ctx_1024P = jax.random.normal(jax.random.fold_in(_rk, 11), (1, 16, 512), jnp.float32)
        _ctx_1024c = jax.random.dirichlet(jax.random.fold_in(_rk, 511), 0.3 * jnp.ones((16,), jnp.float32), (1, 8192))
        _ctx_1024t = jnp.einsum('bsk,bkd->bsd', _ctx_1024c, _ctx_1024P)
        _ctx_1024t = _ctx_1024t * jax.lax.rsqrt(jnp.mean(jnp.square(_ctx_1024t)) + 1e-12) * 0.953939
        ctx_1024 = 4.13588e-05 + 0.999923 * (_ctx_1024t + 0.3 * jax.random.normal(jax.random.fold_in(_rk, 611), (1, 8192, 512), jnp.float32))
        return (x, ctx_1024)
    x, ctx_1024 = _rec_inputs()

    def _L0_xattn_setup():
        import jax, jax.numpy as jnp
        import numpy as np
        D_MODEL = 512
        NHEAD = 16
        key = jax.random.key(seed)
        ks = jax.random.split(key, 11)
        B, S, D = (4, 1024, D_MODEL)
        scale = 1.0 / np.sqrt(D)
        inp = {'q': jax.random.normal(ks[0], (B, S, D), jnp.float32), 'k': jax.random.normal(ks[1], (B, S, D), jnp.float32), 'v': jax.random.normal(ks[2], (B, S, D), jnp.float32), 'Wq': jax.random.normal(ks[3], (D, D), jnp.float32) * scale, 'bq': jnp.zeros((D,), jnp.float32), 'Wk': jax.random.normal(ks[4], (D, D), jnp.float32) * scale, 'bk': jnp.zeros((D,), jnp.float32), 'Wv': jax.random.normal(ks[5], (D, D), jnp.float32) * scale, 'bv': jnp.zeros((D,), jnp.float32), 'Wo': jax.random.normal(ks[6], (D, D), jnp.float32) * scale, 'bo': jnp.zeros((D,), jnp.float32)}
        return inp
    _L0_xattn_all = _L0_xattn_setup()
    _L0_xattn_in = {k: v for k, v in _L0_xattn_all.items() if k in ('Wq', 'bq', 'Wk', 'bk', 'Wv', 'bv', 'Wo', 'bo')}
    del _L0_xattn_all

    def _L0_attn_setup():
        import jax, jax.numpy as jnp
        import numpy as np
        DIM = 512
        HEADS = 16
        DHEAD = DIM // HEADS
        EPS_NORM = 1e-06
        EPS_DEN = 1e-06

        def rmsnorm(x, w):
            xf = x.astype(jnp.float32)
            return (w * xf * jax.lax.rsqrt(jnp.mean(xf * xf, axis=-1, keepdims=True) + EPS_NORM)).astype(x.dtype)
        key = jax.random.key(seed)
        ks = jax.random.split(key, 6)
        b, n = (4, 2048)
        x = jax.random.normal(ks[0], (b, n, DIM), dtype=jnp.float32)
        W_qkv = jax.random.normal(ks[1], (DIM, 3 * DIM), dtype=jnp.float32) * DIM ** (-0.5)
        qn_w = jnp.ones((DIM,), dtype=jnp.float32)
        kn_w = jnp.ones((DIM,), dtype=jnp.float32)
        W_out = jax.random.normal(ks[2], (DIM, DIM), dtype=jnp.float32) * DIM ** (-0.5)
        b_out = jnp.zeros((DIM,), dtype=jnp.float32)
        return {'x': x, 'W_qkv': W_qkv, 'qn_w': qn_w, 'kn_w': kn_w, 'W_out': W_out, 'b_out': b_out}
    _L0_attn_all = _L0_attn_setup()
    _L0_attn_in = {k: v for k, v in _L0_attn_all.items() if k in ('W_qkv', 'qn_w', 'kn_w', 'W_out', 'b_out')}
    del _L0_attn_all

    def _L0_ffn_setup():
        import jax, jax.numpy as jnp
        import numpy as np
        from jax import lax
        H = 512
        E = 8
        E_MLP = E - 4
        TOP_K = 2
        I = 256
        KC = 4
        SHARED_SCALE = 1.0
        key = jax.random.key(seed)
        ks = jax.random.split(key, 8)
        B, S = (4, 2048)
        s_h = 1.0 / np.sqrt(H)
        s_i = 1.0 / np.sqrt(I)
        return {'hidden_states': jax.random.normal(ks[0], (B, S, H), dtype=jnp.float32), 'Wr': jax.random.normal(ks[1], (H, E), dtype=jnp.float32) * s_h, 'router_bias': jnp.zeros((E,), dtype=jnp.float32), 'Wg': jax.random.normal(ks[2], (E_MLP, H, I), dtype=jnp.float32) * s_h, 'Wu': jax.random.normal(ks[3], (E_MLP, H, I), dtype=jnp.float32) * s_h, 'Wd': jax.random.normal(ks[4], (E_MLP, I, H), dtype=jnp.float32) * s_i, 'conv_w': jax.random.normal(ks[5], (KC, 1, H), dtype=jnp.float32) * (1.0 / np.sqrt(KC)), 'conv_b': jnp.zeros((H,), dtype=jnp.float32)}
    _L0_ffn_all = _L0_ffn_setup()
    _L0_ffn_in = {k: v for k, v in _L0_ffn_all.items() if k in ('Wr', 'router_bias', 'Wg', 'Wu', 'Wd', 'conv_w', 'conv_b')}
    del _L0_ffn_all
    return {'x': x, 'ctx_1024': ctx_1024, 'L0_xattn_Wq': _L0_xattn_in['Wq'], 'L0_xattn_bq': _L0_xattn_in['bq'], 'L0_xattn_Wk': _L0_xattn_in['Wk'], 'L0_xattn_bk': _L0_xattn_in['bk'], 'L0_xattn_Wv': _L0_xattn_in['Wv'], 'L0_xattn_bv': _L0_xattn_in['bv'], 'L0_xattn_Wo': _L0_xattn_in['Wo'], 'L0_xattn_bo': _L0_xattn_in['bo'], 'L0_attn_W_qkv': _L0_attn_in['W_qkv'], 'L0_attn_qn_w': _L0_attn_in['qn_w'], 'L0_attn_kn_w': _L0_attn_in['kn_w'], 'L0_attn_W_out': _L0_attn_in['W_out'], 'L0_attn_b_out': _L0_attn_in['b_out'], 'L0_ffn_Wr': _L0_ffn_in['Wr'], 'L0_ffn_router_bias': _L0_ffn_in['router_bias'], 'L0_ffn_Wg': _L0_ffn_in['Wg'], 'L0_ffn_Wu': _L0_ffn_in['Wu'], 'L0_ffn_Wd': _L0_ffn_in['Wd'], 'L0_ffn_conv_w': _L0_ffn_in['conv_w'], 'L0_ffn_conv_b': _L0_ffn_in['conv_b']}

def reference(x, ctx_1024, L0_xattn_Wq, L0_xattn_bq, L0_xattn_Wk, L0_xattn_bk, L0_xattn_Wv, L0_xattn_bv, L0_xattn_Wo, L0_xattn_bo, L0_attn_W_qkv, L0_attn_qn_w, L0_attn_kn_w, L0_attn_W_out, L0_attn_b_out, L0_ffn_Wr, L0_ffn_router_bias, L0_ffn_Wg, L0_ffn_Wu, L0_ffn_Wd, L0_ffn_conv_w, L0_ffn_conv_b):
    import jax
    import jax.numpy as jnp

    def _L0_xattn_ref(q, k, v, Wq, bq, Wk, bk, Wv, bv, Wo, bo):
        import jax, jax.numpy as jnp
        import numpy as np
        D_MODEL = 512
        NHEAD = 16
        qp = jnp.einsum('bsd,ed->bse', q, Wq) + bq
        kp = jnp.einsum('bsd,ed->bse', k, Wk) + bk
        vp = jnp.einsum('bsd,ed->bse', v, Wv) + bv
        scale = 1.0 / np.sqrt(D_MODEL / NHEAD)
        scores = jnp.einsum('bqd,bkd->bqk', qp, kp) * scale
        attn = jax.nn.softmax(scores, axis=-1)
        out = jnp.einsum('bqk,bkd->bqd', attn, vp)
        return jnp.einsum('bsd,ed->bse', out, Wo) + bo

    def _L0_attn_ref(x, W_qkv, qn_w, kn_w, W_out, b_out):
        import jax, jax.numpy as jnp
        import numpy as np
        DIM = 512
        HEADS = 16
        DHEAD = DIM // HEADS
        EPS_NORM = 1e-06
        EPS_DEN = 1e-06

        def rmsnorm(x, w):
            xf = x.astype(jnp.float32)
            return (w * xf * jax.lax.rsqrt(jnp.mean(xf * xf, axis=-1, keepdims=True) + EPS_NORM)).astype(x.dtype)
        b, n, _ = x.shape
        qkv = x @ W_qkv
        q, k, v = jnp.split(qkv, 3, axis=-1)
        q = rmsnorm(q, qn_w)
        k = rmsnorm(k, kn_w)

        def split_heads(t):
            return t.reshape(b, n, HEADS, DHEAD).transpose(0, 2, 1, 3)
        q, k, v = map(split_heads, (q, k, v))
        q = jax.nn.relu(q).astype(jnp.float32)
        k = jax.nn.relu(k).astype(jnp.float32)
        v = v.astype(jnp.float32)
        kv = jnp.einsum('bhnd,bhne->bhde', k, v)
        out = jnp.einsum('bhnd,bhde->bhne', q, kv)
        k_sum = k.sum(axis=2)
        normalizer = jnp.einsum('bhnd,bhd->bhn', q, k_sum) + EPS_DEN
        out = out / normalizer[..., None]
        out = out.transpose(0, 2, 1, 3).reshape(b, n, DIM)
        return out @ W_out + b_out

    def _L0_ffn_ref(hidden_states, Wr, router_bias, Wg, Wu, Wd, conv_w, conv_b):
        import jax, jax.numpy as jnp
        import numpy as np
        from jax import lax
        H = 512
        E = 8
        E_MLP = E - 4
        TOP_K = 2
        I = 256
        KC = 4
        SHARED_SCALE = 1.0
        B, S, Hd = hidden_states.shape
        T = B * S
        x = hidden_states.reshape(T, Hd)
        scores = jax.nn.sigmoid(x @ Wr)
        _, idx = lax.top_k(scores + router_bias, TOP_K)
        w = jnp.take_along_axis(scores, idx, axis=-1)
        w = w / (jnp.sum(w, axis=-1, keepdims=True) + 1e-09)
        cw = jnp.zeros((T, E), dtype=x.dtype).at[jnp.arange(T)[:, None], idx].add(w)
        g = jnp.einsum('th,ehi->tei', x, Wg)
        u = jnp.einsum('th,ehi->tei', x, Wu)
        hid = jax.nn.silu(g) * u
        mlp_out = jnp.einsum('tei,eih->teh', hid, Wd)
        routed = jnp.einsum('te,teh->th', cw[:, :E_MLP], mlp_out)
        routed = routed + cw[:, E_MLP:E_MLP + 1] * x
        routed = routed + cw[:, E_MLP + 2:E_MLP + 3] * x
        routed = routed + cw[:, E_MLP + 3:E_MLP + 4] * jax.nn.relu(x)
        routed = routed.reshape(B, S, Hd)
        shared = lax.conv_general_dilated(hidden_states, conv_w, window_strides=(1,), padding=[(KC - 1, 0)], dimension_numbers=('NHC', 'HIO', 'NHC'), feature_group_count=Hd) + conv_b
        return routed + SHARED_SCALE * shared
    x = x + _L0_xattn_ref(_layernorm(x, axis=-1), ctx_1024, ctx_1024, L0_xattn_Wq, L0_xattn_bq, L0_xattn_Wk, L0_xattn_bk, L0_xattn_Wv, L0_xattn_bv, L0_xattn_Wo, L0_xattn_bo)
    x = x + _L0_attn_ref(_layernorm(x, axis=-1), L0_attn_W_qkv, L0_attn_qn_w, L0_attn_kn_w, L0_attn_W_out, L0_attn_b_out)
    x = x + _L0_ffn_ref(_layernorm(x, axis=-1), L0_ffn_Wr, L0_ffn_router_bias, L0_ffn_Wg, L0_ffn_Wu, L0_ffn_Wd, L0_ffn_conv_w, L0_ffn_conv_b)
    return x

_drawn_inputs = setup_inputs


def setup_inputs(seed=0):
    import zlib

    import numpy as np

    out = dict(_drawn_inputs(seed))
    spreads = {'L0_xattn_bq': (0.0, 0.1),
     'L0_xattn_bk': (0.0, 0.8),
     'L0_xattn_bv': (0.0, 0.1),
     'L0_xattn_bo': (0.0, 0.1),
     'L0_attn_qn_w': (1.0, 0.6),
     'L0_attn_kn_w': (1.0, 0.6),
     'L0_attn_b_out': (0.0, 0.1),
     'L0_ffn_router_bias': (0.0, 0.1),
     'L0_ffn_conv_b': (0.0, 0.1)}
    factors = {}
    for name, (base, spread) in spreads.items():
        noise = np.random.default_rng([zlib.crc32(name.encode()), seed]).standard_normal(out[name].shape)
        drawn = base * np.exp(spread * noise) if base else spread * noise
        out[name] = jnp.asarray(drawn.astype(out[name].dtype))
    for name, factor in factors.items():
        out[name] = (out[name] * factor).astype(out[name].dtype)
    return out
```

```python
from contextlib import ExitStack

import concourse.bass as bass
from concourse import mybir

ALU = mybir.AluOpType
ACT = mybir.ActivationFunctionType
AX = mybir.AxisListType
F32 = mybir.dt.float32
F32R = mybir.dt.float32r

P = 128
D = 512
C = D // P
T = 512
TT = T // P
KEYS = 8192
KB = 512
NB = KEYS // KB
KC = KB // P
STEPS = NB * TT
GROUP = 2 * TT
GROUPS = STEPS // GROUP
SCALE = float(D // 16) ** -0.5
LN_EPS = 1e-5
RMS_EPS = 1e-6
DEN_EPS = 1e-6
TOP_EPS = 1e-9
DH = 32
HG = P // DH
VW = P + HG
E = 8
EM = 4
HID = 256
IC = HID // P
M = EM * IC
TAPS = 4
PAD = TAPS - 1
LOWEST = -3.0e38
ARENA = 184
PIECE = C * HID
PIECES = [("g", 0), ("u", 0), ("g", 1), ("u", 1), ("d", 0), ("g", 2), ("u", 2), ("d", 1), ("g", 3), ("u", 3),
          ("d", 2), ("d", 3)]

COLS = {}
NCOLS = 0
for _name, _n in (("bq", C), ("bk", C), ("bv", C), ("qn", C), ("conv_b", C), ("conv_w", C * TAPS), ("wr", C * E)):
    COLS[_name] = NCOLS
    NCOLS += _n
ROWS = {"bo": (0, D), "kn": (D, 2 * D), "b_out": (2 * D, 3 * D), "rb": (3 * D, 3 * D + E)}
NROWS = 3 * D + E


def perceiver_block(nc, x, ctx_t, ctx_n, wq_t, wk_in, wv_t, wo_t, wqkv_in, wout_in, pieces, cols_in, rows_in, out):
    with ExitStack() as stack:
        def sb(name, shape, dt=F32, on=stack):
            return on.enter_context(nc.sbuf_tensor(name, shape, dt))

        def sem(name):
            return stack.enter_context(nc.semaphore(name))

        bank = stack.enter_context(nc.psum_tensor("bank", [P, 8, 512], F32))

        ident = sb("ident", [P, P])
        cols = sb("cols", [P, NCOLS])
        rows = sb("rows", [P, NROWS])
        xs = sb("xs", [P, TT, D])
        xn = sb("xn", [P, TT, D])
        stats = sb("stats", [P, TT, 6])
        mv = sb("mv", [P, TT, 2])
        var = sb("var", [P, TT])
        std = sb("std", [P, TT])
        rstd = sb("rstd", [P, TT])
        arena = sb("arena", [P, ARENA * 256])
        base = nc.sbuf_base - ARENA * 1024

        def col(name, i):
            a = COLS[name] + i
            return cols[:, a:a + 1]

        def row(name):
            a, b = ROWS[name]
            return rows[:, a:b]

        def at(kib, name, shape, dt=F32):
            size = 4
            for n in shape[1:]:
                size *= n
            assert kib * 1024 + size <= ARENA * 1024
            return nc.alloc_sbuf_tensor_at(name, shape, dt, offset=base + int(kib * 1024))

        def parts(kib, name, shape):
            size = 4
            for n in shape[1:]:
                size *= n
            return at(kib, name + "_h", shape, F32R), at(kib + size / 1024, name + "_l", shape, F32R)

        xT = parts(0, "xT", [P, C, T])
        wq = parts(16, "wq", [P, C, D])
        wk = parts(32, "wk", [P, C, D])
        wq_raw = at(144, "wq_raw", [P, C, D])
        wk_raw = at(152, "wk_raw", [P, C, D])
        qT = parts(144, "qT", [P, C, T])
        q_full = at(164, "q_full", [P, C, T])
        wv_raw = at(0, "wv_raw", [P, C, D])
        wo_raw = at(8, "wo_raw", [P, C, D])
        wv = parts(16, "wv", [P, C, D])
        wo = parts(32, "wo", [P, C, D])
        qk = parts(48, "qk", [P, C, T])
        raw_t = [at(64 + 8 * b, f"raw_t{b}", [P, C, KB]) for b in range(2)]
        raw_n = [at(80 + 8 * b, f"raw_n{b}", [P, KC, D]) for b in range(2)]
        ct = [parts(96 + 16 * b, f"ct{b}", [P, C, KB]) for b in range(2)]
        cn = [parts(128 + 16 * b, f"cn{b}", [P, KC, D]) for b in range(2)]
        probs = [at(160 + 2 * b, f"probs{b}", [P, KB]) for b in range(2)]
        pt = [parts(164 + 4 * b, f"pt{b}", [P, KC, P]) for b in range(2)]
        acc = xn
        small = at(175.5, "small", [P, 11 * TT])

        def stat(n, width=1):
            return small[:, n * TT:(n + width) * TT]

        run_max = stat(0, 2).rearrange("p (m t) -> p m t", m=2)
        block_max, neg_max, exp_bias, key_bias, alpha, row_sum, den, inv_den = (stat(n) for n in range(2, 10))
        kvmask = at(172.5, "kvmask", [P, VW])
        lower = at(173.25, "lower", [P, E, E])
        select = at(173.5, "select", [E, EM, P])
        wqkv = [ct[0], cn[0], ct[1]]
        wout = cn[1]
        vT = parts(48, "vT", [P, C, T])
        square = at(48, "square", [P, D])
        qs = at(64, "qs", [P, TT, D])
        ks = at(72, "ks", [P, TT, D])
        vs = at(80, "vs", [P, TT, C, VW])
        qrT = at(160, "qrT", [P, C, T])
        kv = at(168.25, "kv", [P, C, VW])
        heads = qs
        late = at(62, "late", [P, 512])

        def late_stat(a, *dims):
            n = 1
            for d in dims:
                n *= d
            v = late[:, a:a + n]
            names = " ".join("abc"[:len(dims)])
            sizes = {"abc"[i]: dims[i] for i in range(len(dims))}
            return v.rearrange(f"p ({names}) -> p {names}", **sizes) if len(dims) > 1 else v

        ssq = late_stat(0, TT, 2)
        rms = late_stat(8, TT, 2)
        rrms = late_stat(16, TT, 2)
        norm = late_stat(32, TT, C, HG)
        rnorm = late_stat(96, TT, C, HG)
        sig = late_stat(160, TT, E)
        biased = late_stat(192, TT, E)
        rank = late_stat(224, TT, E)
        gate = late_stat(256, TT, E)
        cw = late_stat(288, TT, E)
        gsum = late_stat(320, TT)
        grec = late_stat(324, TT)
        cw_id = late_stat(328, TT)
        piece_raw = [at(176 + 4 * b, f"piece_raw{b}", [P, PIECE]) for b in range(2)]
        piece = [parts(k, f"piece{n}", [P, PIECE]) for n, k in enumerate((16, 24, 32, 40, 96, 104, 112, 120, 128, 136, 144, 152))]
        order = {(kind, e): n for n, (kind, e) in enumerate(PIECES)}
        xf = at(160, "xf", [P, C, PAD + T])
        cwT = at(168.25, "cwT", [E, T])
        above = at(170.25, "above", [P, TT, E, E])
        tied = at(171.25, "tied", [P, TT, E, E])
        conv = at(48, "conv", [P, C, T])
        relu_x = at(56, "relu_x", [P, 2, D])
        hid = [parts(64 + 4 * b, f"hid{b}", [P, T]) for b in range(3)]
        hid_full = [at(76 + 2 * b, f"hid_full{b}", [P, T]) for b in range(2)]
        act_g = [at(80 + 2 * b, f"act_g{b}", [P, T]) for b in range(2)]
        gu = [at(84 + 2 * b, f"gu{b}", [P, T]) for b in range(2)]
        cwB = at(88, "cwB", [P, EM, T])

        x_loaded = [sem(f"x_loaded{t}") for t in range(TT)]
        cols_loaded = sem("cols_loaded")
        rows_loaded = sem("rows_loaded")
        wq_loaded = sem("wq_loaded")
        wk_loaded = sem("wk_loaded")
        wv_loaded = sem("wv_loaded")
        wo_loaded = sem("wo_loaded")
        piece_loaded = [sem(f"piece_loaded{b}") for b in range(2)]
        piece_high = sem("piece_high")
        piece_ready = sem("piece_ready")
        wq_high = sem("wq_high")
        wq_ready = sem("wq_ready")
        wk_high = sem("wk_high")
        wk_ready = sem("wk_ready")
        wvo_high = sem("wvo_high")
        wvo_ready = sem("wvo_ready")
        raw_loaded = [sem(f"raw_loaded{b}") for b in range(2)]
        out_stored = sem("out_stored")

        ident_ready = sem("ident_ready")
        pads_ready = sem("pads_ready")
        masks_ready = sem("masks_ready")
        bo_added = sem("bo_added")
        ln_step = sem("ln_step")
        var_ready = sem("var_ready")
        std_ready = sem("std_ready")
        xn_ready = sem("xn_ready")
        xnT_psum = sem("xnT_psum")
        xh_ready = sem("xh_ready")
        xl_ready = sem("xl_ready")
        xf_ready = sem("xf_ready")
        q_psum = sem("q_psum")
        qTh_ready = sem("qTh_ready")
        qTl_ready = sem("qTl_ready")
        qfull_ready = sem("qfull_ready")
        qk_psum = sem("qk_psum")
        qkh_ready = sem("qkh_ready")
        qkl_ready = sem("qkl_ready")
        keyb_psum = sem("keyb_psum")
        init_done = sem("init_done")

        ctxh_ready = sem("ctxh_ready")
        ctxl_ready = sem("ctxl_ready")
        s_done = sem("s_done")
        max_step = sem("max_step")
        bias_ready = sem("bias_ready")
        exp_done = sem("exp_done")
        alpha_ready = sem("alpha_ready")
        t_done = sem("t_done")
        pth_ready = sem("pth_ready")
        ptl_ready = sem("ptl_ready")
        pv_done = sem("pv_done")
        acc_done = sem("acc_done")
        den_done = sem("den_done")
        inv_ready = sem("inv_ready")

        v_psum = sem("v_psum")
        vTh_ready = sem("vTh_ready")
        vTl_ready = sem("vTl_ready")
        y_psum = sem("y_psum")
        x1_ready = sem("x1_ready")
        bout_added = sem("bout_added")
        q2_psum = sem("q2_psum")
        k2_psum = sem("k2_psum")
        v2_psum = sem("v2_psum")
        q_ssq = sem("q_ssq")
        k_ssq = sem("k_ssq")
        ms_ready = sem("ms_ready")
        rms_ready = sem("rms_ready")
        rrms_ready = sem("rrms_ready")
        qs_ready = sem("qs_ready")
        kw_ready = sem("kw_ready")
        k_ready = sem("k_ready")
        v_ready = sem("v_ready")
        qsT_psum = sem("qsT_psum")
        qrT_ready = sem("qrT_ready")
        kv_psum = sem("kv_psum")
        kv_ready = sem("kv_ready")
        la_psum = sem("la_psum")
        norm_ready = sem("norm_ready")
        rnorm_ready = sem("rnorm_ready")
        heads_ready = sem("heads_ready")
        z_psum = sem("z_psum")
        x2_ready = sem("x2_ready")
        route_psum = sem("route_psum")
        sig_ready = sem("sig_ready")
        route_step = sem("route_step")
        cw_ready = sem("cw_ready")
        cwT_psum = sem("cwT_psum")
        cwT_ready = sem("cwT_ready")
        cwB_psum = sem("cwB_psum")
        cwB_ready = sem("cwB_ready")
        relu_ready = sem("relu_ready")
        relu_added = sem("relu_added")
        id_added = sem("id_added")
        conv_step = sem("conv_step")
        conv_ready = sem("conv_ready")
        g_psum = sem("g_psum")
        u_psum = sem("u_psum")
        silu_ready = sem("silu_ready")
        gu_ready = sem("gu_ready")
        hid_full_ready = sem("hid_full_ready")
        hidh_ready = sem("hidh_ready")
        hid_ready = sem("hid_ready")
        down_done = sem("down_done")
        o_psum = sem("o_psum")
        out_ready = sem("out_ready")

        def wait(eng, s, n):
            if isinstance(n, int) and n <= 0:
                return
            eng.wait_ge(s, n)

        def over_steps(eng, step, drain):
            for i in range(GROUP):
                step(i, i)
            with eng.Fori(1, GROUPS - 1) as g:
                for u in range(GROUP):
                    step(g * GROUP + u, u)
            for u in range(GROUP):
                step(STEPS - GROUP + u, u, last=True)
            for u in range(drain):
                step(STEPS + u, u, last=True)

        block = stack.enter_context(nc.Block())

        @block.sync
        def _(sp):
            for t in range(TT):
                sp.dma_start(xs[:, t, :], x[t]).then_inc(x_loaded[t], 16)
            sp.dma_start(cols[:], cols_in).then_inc(cols_loaded, 16)
            sp.dma_start(wq_raw[:], wq_t).then_inc(wq_loaded, 16)
            sp.dma_start(wk_raw[:], wk_in).then_inc(wk_loaded, 16)
            for b in range(2):
                sp.dma_start(raw_t[b][:], ctx_t[b]).then_inc(raw_loaded[b], 16)
                sp.dma_start(raw_n[b][:], ctx_n[b]).then_inc(raw_loaded[b], 16)
            sp.dma_start(rows[:], rows_in.partition_broadcast(P)).then_inc(rows_loaded, 16)
            for n in range(2):
                sp.dma_start(piece_raw[n][:], pieces[n]).then_inc(piece_loaded[n], 16)
            sp.wait_ge(q_psum, C)
            sp.dma_start(wv_raw[:], wv_t).then_inc(wv_loaded, 16)
            sp.dma_start(wo_raw[:], wo_t).then_inc(wo_loaded, 16)
            with sp.Fori(1, NB // 2) as g:
                for b in range(2):
                    sp.wait_ge(ctxl_ready, g * (2 * TT) + (b - 1) * TT)
                    sp.dma_start(raw_t[b][:], ctx_t[bass.ds(g * 2 + b, 1)].rearrange("a p c k -> (a p) c k")).then_inc(raw_loaded[b], 16)
                    sp.dma_start(raw_n[b][:], ctx_n[bass.ds(g * 2 + b, 1)].rearrange("a p c k -> (a p) c k")).then_inc(raw_loaded[b], 16)
            for b in range(2):
                sp.wait_ge(ctxl_ready, (NB - 1 + b) * TT)
                sp.dma_start(raw_t[b][:], wqkv_in[2 * b]).then_inc(raw_loaded[b], 16)
                sp.dma_start(raw_n[b][:], wqkv_in[1] if b == 0 else wout_in).then_inc(raw_loaded[b], 16)
            for n in range(2, len(PIECES)):
                sp.wait_ge(piece_ready, n - 1)
                sp.dma_start(piece_raw[n % 2][:], pieces[n]).then_inc(piece_loaded[n % 2], 16)
            for t in range(TT):
                sp.wait_ge(out_ready, t + 1)
                sp.dma_start(out[t], xs[:, t, :]).then_inc(out_stored, 16)
            sp.wait_ge(out_stored, 16 * TT)

        @block.gpsimd
        def _(pool):
            pool.memset(ident[:], 0.0).then_inc(ident_ready, 1)
            pool.wait_ge(ident_ready, 1)
            pool.affine_select(out=ident[:], in_=ident[:], compare_op=ALU.not_equal, fill=1.0, base=0,
                               pattern=[[-1, P]], channel_multiplier=1).then_inc(ident_ready, 1)
            pool.wait_ge(wk_loaded, 16)
            pool.tensor_copy(wk[0][:], wk_raw[:]).then_inc(wk_high, 1)
            pool.wait_ge(wk_high, 1)
            pool.tensor_tensor(wk[1][:], wk_raw[:], wk[0][:].bitcast(F32), ALU.subtract).then_inc(wk_ready, 1)
            pool.wait_ge(rows_loaded, 16)
            pool.wait_ge(xn_ready, TT)
            for t in range(TT):
                pool.tensor_tensor(xs[:, t, :], xs[:, t, :], row("bo"), ALU.add).then_inc(bo_added, 1)
            pool.wait_ge(qk_psum, C)
            for n, (raw, w, loaded) in enumerate(((wv_raw, wv, wv_loaded), (wo_raw, wo, wo_loaded))):
                pool.wait_ge(loaded, 16)
                pool.tensor_copy(w[0][:], raw[:]).then_inc(wvo_high, 1)
                pool.wait_ge(wvo_high, n + 1)
                pool.tensor_tensor(w[1][:], raw[:], w[0][:].bitcast(F32), ALU.subtract).then_inc(wvo_ready, 1)
            pool.memset(kvmask[:], 0.0).then_inc(masks_ready, 1)
            pool.memset(lower[:], 0.0).then_inc(masks_ready, 1)
            pool.memset(select[:], 0.0).then_inc(masks_ready, 1)
            pool.wait_ge(masks_ready, 3)
            made = 3
            for h in range(HG):
                pool.memset(kvmask[h * DH:(h + 1) * DH, h * DH:(h + 1) * DH], 1.0).then_inc(masks_ready, 1)
                made += 1
                pool.wait_ge(masks_ready, made)
                pool.memset(kvmask[h * DH:(h + 1) * DH, P + h:P + h + 1], 1.0).then_inc(masks_ready, 1)
                made += 1
                pool.wait_ge(masks_ready, made)
            for e in range(1, E):
                pool.memset(lower[:, e, 0:e], 1.0).then_inc(masks_ready, 1)
                made += 1
                pool.wait_ge(masks_ready, made)
            for e in range(EM):
                pool.affine_select(out=select[:, e, :], in_=select[:, e, :], compare_op=ALU.not_equal, fill=1.0,
                                   base=-e, pattern=[[0, P]], channel_multiplier=1).then_inc(masks_ready, 1)
                made += 1
                pool.wait_ge(masks_ready, made)
            pool.wait_ge(ctxl_ready, (NB + 2) * TT)
            pool.memset(vs[:, :, :, P:VW], 1.0).then_inc(pads_ready, 1)

            def split_piece(n):
                pool.wait_ge(piece_loaded[n % 2], 16 * (n // 2 + 1))
                pool.tensor_copy(piece[n][0][:], piece_raw[n % 2][:]).then_inc(piece_high, 1)
                pool.wait_ge(piece_high, n + 1)
                pool.tensor_tensor(piece[n][1][:], piece_raw[n % 2][:], piece[n][0][:].bitcast(F32),
                                   ALU.subtract).then_inc(piece_ready, 1)

            pool.wait_ge(y_psum, TT)
            for n in range(0, 4):
                split_piece(n)
            pool.wait_ge(xn_ready, 3 * TT)
            for t in range(TT):
                pool.tensor_tensor(xs[:, t, :], xs[:, t, :], row("b_out"), ALU.add).then_inc(bout_added, 1)
            pool.wait_ge(v2_psum, TT)
            for n in range(4, 8):
                split_piece(n)
            pool.wait_ge(la_psum, 2 * TT)
            pool.memset(xf[:, :, 0:PAD], 0.0).then_inc(pads_ready, 1)
            for n in range(8, 10):
                split_piece(n)
            pool.wait_ge(cw_ready, 1)
            for t in range(TT):
                wait(pool, relu_added, t - 1)
                pool.tensor_scalar(relu_x[:, t % 2, :], xn[:, t, :], 0.0, cw[:, t, 7:8], ALU.max, ALU.mult).then_inc(relu_ready, 1)
                pool.wait_ge(relu_ready, t + 1)
                pool.tensor_tensor(xs[:, t, :], xs[:, t, :], relu_x[:, t % 2, :], ALU.add).then_inc(relu_added, 1)
            pool.wait_ge(z_psum, TT)
            for n in range(10, 12):
                split_piece(n)

        MASKS = 3 + 2 * HG + E - 1 + EM

        @block.scalar
        def _(act):
            def std_of(n):
                t = n % TT
                act.wait_ge(var_ready, n + 1)
                act.activation(std[:, t:t + 1], var[:, t:t + 1], ACT.Sqrt).then_inc(std_ready, 1)

            def high_xT(n, first_bank):
                t = n % TT
                act.wait_ge(xnT_psum, n + 1)
                act.copy(xT[0][:, :, t * P:(t + 1) * P],
                         bank[:, first_bank + t, :].rearrange("p (c t) -> p c t", c=C)).then_inc(xh_ready, 1)

            act.wait_ge(wq_loaded, 16)
            act.copy(wq[0][:], wq_raw[:]).then_inc(wq_high, 1)
            for t in range(TT):
                std_of(t)
            for t in range(TT):
                high_xT(t, 0)

            act.wait_ge(raw_loaded[0], 32)
            for u in range(TT):
                src, dst = (raw_t[0], ct[0][0]) if u < 2 else (raw_n[0], cn[0][0])
                v = 2 * (u % 2)
                act.copy(dst[:, v:v + 2, :], src[:, v:v + 2, :]).then_inc(ctxh_ready, 1)
            act.wait_ge(cols_loaded, 16)
            act.wait_ge(wq_ready, 1)
            act.wait_ge(wk_ready, 1)
            for c in range(C):
                act.wait_ge(q_psum, c + 1)
                act.activation(qT[0][:, c, :], bank[:, 4 + c, :], ACT.Identity, bias=col("bq", c)).then_inc(qTh_ready, 1)
            for c in range(C):
                act.wait_ge(qk_psum, c + 1)
                act.copy(qk[0][:, c, :], bank[:, c, :]).then_inc(qkh_ready, 1)

            def step(i, u, last=False):
                if not (isinstance(i, int) and i == 0):
                    b = (u - 1) % 2
                    wait(act, t_done, i)
                    wait(act, pv_done, i - 2)
                    act.copy(pt[b][0][:], bank[:, 2 + b, :].rearrange("p (c k) -> p c k", c=KC)).then_inc(pth_ready, 1)
                if isinstance(i, int) and i >= STEPS:
                    return
                t, b, m = u % TT, u % 2, (u // TT) % 2
                act.wait_ge(bias_ready, i + 1)
                act.activation(probs[b][:], bank[:, b, :], ACT.Exp, bias=exp_bias[:, t:t + 1], scale=SCALE,
                               accum_out=row_sum[:, t:t + 1]).then_inc(exp_done, 1)
                act.activation(alpha[:, t:t + 1], run_max[:, m, t:t + 1], ACT.Exp, bias=neg_max[:, t:t + 1],
                               scale=SCALE).then_inc(alpha_ready, 1)
                next_high(i, t, 1 - m)

            def next_high(i, t, nb):
                if t == 0:
                    act.wait_ge(raw_loaded[nb], (i + TT - nb * TT) * 4 + 32)
                if t < 2:
                    wait(act, s_done, i - t)
                    act.copy(ct[nb][0][:, 2 * t:2 * t + 2, :], raw_t[nb][:, 2 * t:2 * t + 2, :]).then_inc(ctxh_ready, 1)
                else:
                    v = 2 * (t - 2)
                    wait(act, pv_done, i - t)
                    act.copy(cn[nb][0][:, v:v + 2, :], raw_n[nb][:, v:v + 2, :]).then_inc(ctxh_ready, 1)

            over_steps(act, step, 1)

            for t in range(TT):
                next_high(STEPS + t, t, 1)
            act.wait_ge(wvo_ready, 2)
            for t in range(TT):
                high_xT(TT + t, 0)
            for c in range(C):
                act.wait_ge(v_psum, c + 1)
                act.activation(vT[0][:, c, :], bank[:, 4 + c, :], ACT.Identity, bias=col("bv", c)).then_inc(vTh_ready, 1)
            for t in range(TT):
                std_of(TT + t)
            for t in range(TT):
                high_xT(2 * TT + t, 4)
            act.wait_ge(ctxl_ready, (NB + 2) * TT)
            for t in range(TT):
                act.wait_ge(q2_psum, t + 1)
                act.activation(square[:], bank[:, (3 * t) % 8, :], ACT.Square, accum_out=ssq[:, t, 0:1]).then_inc(q_ssq, 1)
                act.wait_ge(q_ssq, 2 * t + 1)
                act.wait_ge(k2_psum, t + 1)
                act.activation(square[:], bank[:, (3 * t + 1) % 8, :], ACT.Square, accum_out=ssq[:, t, 1:2]).then_inc(q_ssq, 1)
                act.wait_ge(v2_psum, t + 1)
                act.copy(vs[:, t, :, 0:P], bank[:, (3 * t + 2) % 8, :].rearrange("p (c k) -> p c k", c=C)).then_inc(v_ready, 1)
                act.wait_ge(ms_ready, t + 1)
                act.activation(rms[:, t, :], rms[:, t, :], ACT.Sqrt).then_inc(rms_ready, 1)
                act.wait_ge(rrms_ready, t + 1)
                act.activation(qs[:, t, :], bank[:, (3 * t) % 8, :], ACT.Copy, scale=rrms[:, t, 0:1]).then_inc(qs_ready, 1)
            for c in range(C):
                act.wait_ge(qsT_psum, c + 1)
                act.activation(qrT[:, c, :], bank[:, 4 + c, :], ACT.Relu, scale=col("qn", c)).then_inc(qrT_ready, 1)
            for t in range(TT):
                high_xT(3 * TT + t, 0)
            for t in range(TT):
                std_of(2 * TT + t)
            for t in range(TT):
                high_xT(4 * TT + t, 0)
                act.wait_ge(xl_ready, 4 * TT + t + 1)
                act.copy(xf[:, :, PAD + t * P:PAD + (t + 1) * P],
                         bank[:, t, :].rearrange("p (c t) -> p c t", c=C)).then_inc(xf_ready, 1)

            def high_hid(m):
                act.wait_ge(hid_full_ready, m + 1)
                wait(act, down_done, m - 2)
                act.copy(hid[m % 3][0][:], hid_full[m % 2][:]).then_inc(hidh_ready, 1)

            act.wait_ge(route_psum, 1)
            act.activation(sig[:].rearrange("p t e -> p (t e)"), bank[:, 4, 0:TT * E], ACT.Sigmoid).then_inc(sig_ready, 1)
            for m in range(M):
                if m == 1:
                    act.wait_ge(cwT_psum, 1)
                    act.copy(cwT[:], bank[0:E, 5, :]).then_inc(cwT_ready, 1)
                    for e in range(EM):
                        act.wait_ge(cwB_psum, e + 1)
                        act.copy(cwB[:, e, :], bank[:, 4 + e, :]).then_inc(cwB_ready, 1)
                act.wait_ge(g_psum, m + 1)
                wait(act, gu_ready, m - 1)
                act.activation(act_g[m % 2][:], bank[:, m % 2, :], ACT.Silu).then_inc(silu_ready, 1)
                if m >= 1:
                    high_hid(m - 1)
            high_hid(M - 1)

        @block.vector
        def _(dve):
            lnc = [0]

            def ln_chain(ins):
                ins.then_inc(ln_step, 1)
                lnc[0] += 1
                dve.wait_ge(ln_step, lnc[0])

            def ln_stats(n):
                t = n % TT
                ln_chain(dve.bn_stats(stats[:, t, :], xs[:, t, :]))
                ln_chain(dve.bn_aggr(mv[:, t, :], stats[:, t, :]))
                dve.tensor_scalar(var[:, t:t + 1], mv[:, t, 1:2], LN_EPS, None, ALU.add).then_inc(var_ready, 1)

            def ln_apply(n):
                t = n % TT
                dve.wait_ge(std_ready, n + 1)
                ln_chain(dve.reciprocal(rstd[:, t:t + 1], std[:, t:t + 1]))
                dve.tensor_scalar(xn[:, t, :], xs[:, t, :], mv[:, t, 0:1], rstd[:, t:t + 1], ALU.subtract,
                                  ALU.mult).then_inc(xn_ready, 1)

            for t in range(TT):
                dve.wait_ge(x_loaded[t], 16)
                ln_stats(t)
                if t:
                    ln_apply(t - 1)
            ln_apply(TT - 1)

            def low_xT(n, first_bank):
                t = n % TT
                dve.wait_ge(xh_ready, n + 1)
                dve.tensor_tensor(xT[1][:, :, t * P:(t + 1) * P],
                                  bank[:, first_bank + t, :].rearrange("p (c t) -> p c t", c=C),
                                  xT[0][:, :, t * P:(t + 1) * P].bitcast(F32), ALU.subtract).then_inc(xl_ready, 1)

            dve.wait_ge(wq_high, 1)
            dve.tensor_tensor(wq[1][:], wq_raw[:], wq[0][:].bitcast(F32), ALU.subtract).then_inc(wq_ready, 1)
            for t in range(TT):
                low_xT(t, 0)

            def split_low(t, b, q):
                dve.wait_ge(ctxh_ready, q + 1)
                raw, split = (raw_t, ct) if t < 2 else (raw_n, cn)
                v = 2 * (t % 2)
                dve.tensor_tensor(split[b][1][:, v:v + 2, :], raw[b][:, v:v + 2, :],
                                  split[b][0][:, v:v + 2, :].bitcast(F32),
                                  ALU.subtract).then_inc(ctxl_ready, 1)

            for t in range(TT - 1):
                split_low(t, 0, t)
            dve.wait_ge(cols_loaded, 16)
            for c in range(C):
                dve.wait_ge(qTh_ready, c + 1)
                dve.scalar_tensor_tensor(out=qT[1][:, c, :], in0=bank[:, 4 + c, :], scalar=col("bq", c),
                                         in1=qT[0][:, c, :].bitcast(F32), op0=ALU.add, op1=ALU.subtract).then_inc(qTl_ready, 1)
            for c in range(C):
                dve.tensor_scalar(q_full[:, c, :], bank[:, 4 + c, :], col("bq", c), None, ALU.add).then_inc(qfull_ready, 1)
            for c in range(C):
                dve.wait_ge(qkh_ready, c + 1)
                dve.tensor_tensor(qk[1][:, c, :], bank[:, c, :], qk[0][:, c, :].bitcast(F32), ALU.subtract).then_inc(qkl_ready, 1)
            dve.wait_ge(keyb_psum, 1)
            dve.tensor_copy(key_bias[:], bank[:, 4, 0:TT]).then_inc(init_done, 1)
            dve.memset(run_max[:, 0, :], LOWEST).then_inc(init_done, 1)
            dve.memset(den[:], 0.0).then_inc(init_done, 1)
            dve.wait_ge(xnT_psum, TT)
            dve.memset(acc[:], 0.0).then_inc(init_done, 1)
            dve.wait_ge(init_done, 4)

            def step(i, u, last=False):
                if not (isinstance(i, int) and i < 3):
                    t, b = (u - 3) % TT, (u - 3) % 2
                    dve.wait_ge(pv_done, i - 2)
                    dve.wait_ge(alpha_ready, i - 2)
                    wait(dve, den_done, i - 3)
                    dve.scalar_tensor_tensor(out=acc[:, t, :], in0=acc[:, t, :], scalar=alpha[:, t:t + 1],
                                             in1=bank[:, 4 + b, :], op0=ALU.mult, op1=ALU.add).then_inc(acc_done, 1)
                    dve.scalar_tensor_tensor(out=den[:, t:t + 1], in0=den[:, t:t + 1], scalar=alpha[:, t:t + 1],
                                             in1=row_sum[:, t:t + 1], op0=ALU.mult, op1=ALU.add).then_inc(den_done, 1)
                    if last and i - 3 >= STEPS - TT:
                        dve.wait_ge(den_done, i - 2)
                        dve.reciprocal(inv_den[:, t:t + 1], den[:, t:t + 1]).then_inc(inv_ready, 1)
                        dve.wait_ge(inv_ready, t + 1)
                        dve.tensor_scalar(acc[:, t, :], acc[:, t, :], inv_den[:, t:t + 1], None, ALU.mult).then_inc(xn_ready, 1)
                live = not (isinstance(i, int) and i >= STEPS)
                t, b, m = u % TT, u % 2, (u // TT) % 2
                if live:
                    split_low((t - 1) % TT, m if t == 0 else 1 - m, i + 3)
                if live:
                    dve.wait_ge(s_done, i + 1)
                    dve.reduce_max(block_max[:, t:t + 1], bank[:, b, :], AX.X).then_inc(max_step, 1)
                    dve.wait_ge(max_step, i * 2 + 1)
                    dve.tensor_scalar(run_max[:, 1 - m, t:t + 1], block_max[:, t:t + 1], key_bias[:, t:t + 1],
                                      run_max[:, m, t:t + 1], ALU.add, ALU.max).then_inc(max_step, 1)
                    dve.wait_ge(max_step, i * 2 + 2)
                    dve.tensor_scalar(neg_max[:, t:t + 1], run_max[:, 1 - m, t:t + 1], -SCALE, None, ALU.mult)
                    dve.tensor_scalar(exp_bias[:, t:t + 1], run_max[:, 1 - m, t:t + 1], key_bias[:, t:t + 1], -SCALE,
                                      ALU.subtract, ALU.mult).then_inc(bias_ready, 1)
                if not (isinstance(i, int) and (i == 0 or i > STEPS)):
                    b = (u - 1) % 2
                    dve.wait_ge(pth_ready, i)
                    dve.tensor_tensor(pt[b][1][:], bank[:, 2 + b, :].rearrange("p (c k) -> p c k", c=KC),
                                      pt[b][0][:].bitcast(F32), ALU.subtract).then_inc(ptl_ready, 1)

            over_steps(dve, step, 3)

            for t in range(TT):
                low_xT(TT + t, 0)
            split_low(TT - 1, 0, STEPS + TT - 1)
            for t in range(TT):
                split_low(t, 1, STEPS + TT + t)
            for c in range(C):
                dve.wait_ge(vTh_ready, c + 1)
                dve.scalar_tensor_tensor(out=vT[1][:, c, :], in0=bank[:, 4 + c, :], scalar=col("bv", c),
                                         in1=vT[0][:, c, :].bitcast(F32), op0=ALU.add, op1=ALU.subtract).then_inc(vTl_ready, 1)
            dve.wait_ge(bo_added, TT)
            for t in range(TT):
                dve.wait_ge(y_psum, t + 1)
                dve.tensor_tensor(xs[:, t, :], xs[:, t, :], bank[:, t, :], ALU.add).then_inc(x1_ready, 1)
                dve.wait_ge(x1_ready, t + 1)
                dve.wait_ge(xnT_psum, 2 * TT)
                ln_stats(TT + t)
                if t:
                    ln_apply(TT + t - 1)
            ln_apply(2 * TT - 1)
            for t in range(TT):
                low_xT(2 * TT + t, 4)

            for t in range(TT):
                dve.wait_ge(q_ssq, 2 * t + 2)
                dve.tensor_scalar(rms[:, t, :], ssq[:, t, :], 1.0 / D, RMS_EPS, ALU.mult, ALU.add).then_inc(ms_ready, 1)
                dve.wait_ge(rms_ready, t + 1)
                dve.reciprocal(rrms[:, t, :], rms[:, t, :]).then_inc(rrms_ready, 1)
                dve.wait_ge(rrms_ready, t + 1)
                dve.scalar_tensor_tensor(out=ks[:, t, :], in0=bank[:, (3 * t + 1) % 8, :], scalar=rrms[:, t, 1:2],
                                         in1=row("kn"), op0=ALU.mult, op1=ALU.mult).then_inc(kw_ready, 1)
                dve.wait_ge(kw_ready, t + 1)
                dve.tensor_scalar(ks[:, t, :], ks[:, t, :], 0.0, None, ALU.max).then_inc(k_ready, 1)
            dve.wait_ge(masks_ready, MASKS)
            for c in range(C):
                dve.wait_ge(kv_psum, c + 1)
                dve.tensor_tensor(kv[:, c, :], bank[:, c, 0:VW], kvmask[:], ALU.mult).then_inc(kv_ready, 1)
            dve.wait_ge(qsT_psum, C)
            for t in range(TT):
                for half in range(2):
                    n = 2 * t + half
                    dve.wait_ge(la_psum, n + 1)
                    la = bank[:, 4 + n % 4, 0:2 * VW].rearrange("p (g w) -> p g w", g=2)
                    dve.tensor_scalar(norm[:, t, 2 * half:2 * half + 2, :], la[:, :, P:VW], DEN_EPS, None, ALU.add).then_inc(norm_ready, 1)
                    dve.wait_ge(norm_ready, n + 1)
                    dve.reciprocal(rnorm[:, t, 2 * half:2 * half + 2, :], norm[:, t, 2 * half:2 * half + 2, :]).then_inc(rnorm_ready, 1)
                    dve.wait_ge(rnorm_ready, n + 1)
                    for g in range(2):
                        ins = dve.tensor_tensor(
                            heads[:, t, (2 * half + g) * P:(2 * half + g + 1) * P].rearrange("p (h e) -> p h e", h=HG),
                            la[:, g, 0:P].rearrange("p (h e) -> p h e", h=HG),
                            rnorm[:, t, 2 * half + g, :].unsqueeze(2).to_broadcast([P, HG, DH]), ALU.mult)
                    ins.then_inc(heads_ready, 1)
            for t in range(TT):
                low_xT(3 * TT + t, 0)
            for t in range(TT):
                dve.wait_ge(z_psum, t + 1)
                dve.wait_ge(bout_added, t + 1)
                dve.tensor_tensor(xs[:, t, :], xs[:, t, :], bank[:, 4 + t, :], ALU.add).then_inc(x2_ready, 1)
                dve.wait_ge(x2_ready, t + 1)
                ln_stats(2 * TT + t)
                if t:
                    ln_apply(2 * TT + t - 1)
            ln_apply(3 * TT - 1)
            for t in range(TT):
                low_xT(4 * TT + t, 0)

            rc = [0]

            def route(ins):
                ins.then_inc(route_step, 1)
                rc[0] += 1
                dve.wait_ge(route_step, rc[0])

            dve.wait_ge(sig_ready, 1)
            route(dve.tensor_tensor(biased[:], sig[:], row("rb").unsqueeze(1).to_broadcast([P, TT, E]), ALU.add))
            for t in range(TT):
                mine = biased[:, t, :].unsqueeze(2).to_broadcast([P, E, E])
                others = biased[:, t, :].unsqueeze(1).to_broadcast([P, E, E])
                dve.tensor_tensor(above[:, t], others, mine, ALU.is_gt)
                ins = dve.tensor_tensor(tied[:, t], others, mine, ALU.is_equal)
            route(ins)
            route(dve.tensor_tensor(tied[:], tied[:], lower[:].unsqueeze(1).to_broadcast([P, TT, E, E]), ALU.mult))
            route(dve.tensor_tensor(above[:], above[:], tied[:], ALU.add))
            route(dve.reduce_sum(rank[:], above[:], AX.X))
            route(dve.scalar_tensor_tensor(out=gate[:], in0=rank[:], scalar=1.5, in1=sig[:], op0=ALU.is_lt, op1=ALU.mult))
            route(dve.reduce_sum(gsum[:], gate[:], AX.X))
            route(dve.tensor_scalar(gsum[:], gsum[:], TOP_EPS, None, ALU.add))
            route(dve.reciprocal(grec[:], gsum[:]))
            dve.tensor_tensor(cw[:], gate[:], grec[:].unsqueeze(2).to_broadcast([P, TT, E]), ALU.mult).then_inc(cw_ready, 1)
            dve.wait_ge(cw_ready, 1)
            route(dve.tensor_tensor(cw_id[:], cw[:, :, 4], cw[:, :, 6], ALU.add))

            def experts(m):
                dve.wait_ge(silu_ready, m + 1)
                dve.wait_ge(u_psum, m + 1)
                wait(dve, hid_full_ready, m - 1)
                dve.tensor_tensor(gu[m % 2][:], act_g[m % 2][:], bank[:, 2 + m % 2, :], ALU.mult).then_inc(gu_ready, 1)
                dve.wait_ge(gu_ready, m + 1)
                dve.wait_ge(cwB_ready, m // IC + 1)
                wait(dve, hid_ready, m - 1)
                dve.tensor_tensor(hid_full[m % 2][:], gu[m % 2][:], cwB[:, m // IC, :], ALU.mult).then_inc(hid_full_ready, 1)

            def low_hid(m):
                dve.wait_ge(hidh_ready, m + 1)
                dve.tensor_tensor(hid[m % 3][1][:], hid_full[m % 2][:], hid[m % 3][0][:].bitcast(F32),
                                  ALU.subtract).then_inc(hid_ready, 1)

            convc = [0]

            def conv_chain(ins):
                ins.then_inc(conv_step, 1)
                convc[0] += 1
                dve.wait_ge(conv_step, convc[0])

            dve.wait_ge(pads_ready, 2)
            dve.wait_ge(xf_ready, TT)
            for m in range(M):
                experts(m)
                if m >= 1:
                    low_hid(m - 1)
                if m < TT:
                    dve.wait_ge(relu_added, m + 1)
                    dve.scalar_tensor_tensor(out=xs[:, m, :], in0=xn[:, m, :], scalar=cw_id[:, m:m + 1],
                                             in1=xs[:, m, :], op0=ALU.mult, op1=ALU.add).then_inc(id_added, 1)
                if m < C:
                    def tap(j):
                        return cols[:, COLS["conv_w"] + m * TAPS + j:COLS["conv_w"] + m * TAPS + j + 1]

                    conv_chain(dve.tensor_scalar(conv[:, m, :], xf[:, m, 0:T], tap(0), col("conv_b", m), ALU.mult, ALU.add))
                    for j in range(1, TAPS):
                        ins = dve.scalar_tensor_tensor(out=conv[:, m, :], in0=xf[:, m, j:j + T], scalar=tap(j),
                                                       in1=conv[:, m, :], op0=ALU.mult, op1=ALU.add)
                        if j < TAPS - 1:
                            conv_chain(ins)
                    ins.then_inc(conv_ready, 1)
            low_hid(M - 1)
            for t in range(TT):
                dve.wait_ge(o_psum, t + 1)
                dve.wait_ge(id_added, TT)
                dve.tensor_tensor(xs[:, t, :], xs[:, t, :], bank[:, 4 + t, :], ALU.add).then_inc(out_ready, 1)

        @block.tensor
        def _(pe):
            def transpose_tile(src, t, dst):
                for c in range(C):
                    ins = pe.transpose(bank[:, dst, c * P:(c + 1) * P], src[:, t, c * P:(c + 1) * P], ident[:])
                return ins

            def project(dst, lhs, rhs, starts=True, stops=True):
                n = len(lhs)
                for c in range(n):
                    (a_h, a_l), (b_h, b_l) = lhs[c], rhs[c]
                    for k, (a, b) in enumerate(((a_h, b_h), (a_h, b_l), (a_l, b_h))):
                        ins = pe.matmul(bank[:, dst, :], a, b, start=(starts and c == 0 and k == 0),
                                        stop=(stops and c == n - 1 and k == 2))
                return ins

            def cut(w, c, a, b):
                return w[0][:, c, a:b], w[1][:, c, a:b]

            pe.wait_ge(ident_ready, 2)
            for t in range(TT):
                pe.wait_ge(xn_ready, t + 1)
                transpose_tile(xn, t, t).then_inc(xnT_psum, 1)
            pe.wait_ge(xl_ready, TT)
            pe.wait_ge(wq_ready, 1)
            for e in range(C):
                project(4 + e, [cut(wq, c, e * P, (e + 1) * P) for c in range(C)],
                        [cut(xT, c, 0, T) for c in range(C)]).then_inc(q_psum, 1)
            pe.wait_ge(qTl_ready, C)
            pe.wait_ge(wk_ready, 1)
            for c in range(C):
                project(c, [cut(wk, e, c * P, (c + 1) * P) for e in range(C)],
                        [cut(qT, e, 0, T) for e in range(C)]).then_inc(qk_psum, 1)
            pe.wait_ge(cols_loaded, 16)
            pe.wait_ge(qfull_ready, C)
            for t in range(TT):
                for e in range(C):
                    ins = pe.matmul(bank[:, 4, t:t + 1], q_full[:, e, t * P:(t + 1) * P], col("bk", e),
                                    start=(e == 0), stop=(e == C - 1))
            ins.then_inc(keyb_psum, 1)
            pe.wait_ge(qkl_ready, C)

            def scores(i, u):
                t, b, m = u % TT, u % 2, (u // TT) % 2
                if t == 0:
                    pe.wait_ge(ctxl_ready, i + 2)
                wait(pe, exp_done, i - 1)
                ins = project(b, [cut(qk, c, t * P, (t + 1) * P) for c in range(C)],
                              [cut(ct[m], c, 0, KB) for c in range(C)])
                ins.then_inc(s_done, 1)

            def transposes(i, u):
                b = u % 2
                pe.wait_ge(exp_done, i + 1)
                wait(pe, ptl_ready, i - 1)
                for c in range(KC):
                    ins = pe.transpose(bank[:, 2 + b, c * P:(c + 1) * P], probs[b][:, c * P:(c + 1) * P], ident[:])
                ins.then_inc(t_done, 1)

            def weighted_sums(i, u):
                t, b, m = u % TT, u % 2, (u // TT) % 2
                pe.wait_ge(ptl_ready, i + 1)
                if t == 0:
                    pe.wait_ge(ctxl_ready, i + 4)
                wait(pe, acc_done, i - 1)
                ins = project(4 + b, [cut(pt[b], c, 0, P) for c in range(KC)],
                              [cut(cn[m], c, 0, D) for c in range(KC)])
                ins.then_inc(pv_done, 1)

            def step(i, u, last=False):
                if not (isinstance(i, int) and i >= STEPS):
                    scores(i, u)
                if not (isinstance(i, int) and (i < 1 or i > STEPS)):
                    transposes(i - 1, (u - 1) % GROUP)
                if not (isinstance(i, int) and i < 2):
                    weighted_sums(i - 2, (u - 2) % GROUP)

            over_steps(pe, step, 2)

            for t in range(TT):
                pe.wait_ge(xn_ready, TT + t + 1)
                transpose_tile(acc, t, t).then_inc(xnT_psum, 1)
            pe.wait_ge(xl_ready, 2 * TT)
            for e in range(C):
                project(4 + e, [cut(wv, c, e * P, (e + 1) * P) for c in range(C)],
                        [cut(xT, c, 0, T) for c in range(C)]).then_inc(v_psum, 1)
            pe.wait_ge(vTl_ready, C)
            for t in range(TT):
                project(t, [cut(vT, e, t * P, (t + 1) * P) for e in range(C)],
                        [cut(wo, e, 0, D) for e in range(C)]).then_inc(y_psum, 1)

            for t in range(TT):
                pe.wait_ge(xn_ready, 2 * TT + t + 1)
                transpose_tile(xn, t, 4 + t).then_inc(xnT_psum, 1)
            pe.wait_ge(ctxl_ready, (NB + 2) * TT)
            for t in range(TT):
                pe.wait_ge(xl_ready, 2 * TT + t + 1)
                for s, done in enumerate((q2_psum, k2_psum, v2_psum)):
                    n = 3 * t + s
                    if n >= 8:
                        before, tb = (n - 8) % 3, (n - 8) // 3
                        pe.wait_ge((qs_ready, kw_ready, v_ready)[before], tb + 1)
                    if 4 <= n < 8:
                        pe.wait_ge(xl_ready, 3 * TT)
                    project(n % 8, [cut(xT, c, t * P, (t + 1) * P) for c in range(C)],
                            [cut(wqkv[s], c, 0, D) for c in range(C)]).then_inc(done, 1)
            pe.wait_ge(qs_ready, TT)
            pe.wait_ge(kw_ready, TT)
            pe.wait_ge(v_ready, TT)
            for c in range(C):
                for t in range(TT):
                    ins = pe.transpose(bank[:, 4 + c, t * P:(t + 1) * P], qs[:, t, c * P:(c + 1) * P], ident[:])
                ins.then_inc(qsT_psum, 1)
            pe.wait_ge(k_ready, TT)
            pe.wait_ge(pads_ready, 1)
            for c in range(C):
                for t in range(TT):
                    ins = pe.matmul(bank[:, c, 0:VW], ks[:, t, c * P:(c + 1) * P], vs[:, t, c, :],
                                    start=(t == 0), stop=(t == TT - 1))
                ins.then_inc(kv_psum, 1)
            pe.wait_ge(kv_ready, C)
            pe.wait_ge(qrT_ready, C)
            for t in range(TT):
                for half in range(2):
                    n = 2 * t + half
                    wait(pe, heads_ready, n - 3)
                    for g in range(2):
                        c = 2 * half + g
                        ins = pe.matmul(bank[:, 4 + n % 4, g * VW:(g + 1) * VW], qrT[:, c, t * P:(t + 1) * P], kv[:, c, :],
                                        start=True, stop=True)
                    ins.then_inc(la_psum, 1)
            for t in range(TT):
                pe.wait_ge(heads_ready, 2 * t + 2)
                transpose_tile(heads, t, t).then_inc(xnT_psum, 1)
            for t in range(TT):
                pe.wait_ge(xl_ready, 3 * TT + t + 1)
                project(4 + t, [cut(xT, c, t * P, (t + 1) * P) for c in range(C)],
                        [cut(wout, c, 0, D) for c in range(C)]).then_inc(z_psum, 1)

            for t in range(TT):
                pe.wait_ge(xn_ready, 3 * TT + t + 1)
                transpose_tile(xn, t, t).then_inc(xnT_psum, 1)
            pe.wait_ge(xf_ready, TT)
            for t in range(TT):
                for c in range(C):
                    a = COLS["wr"] + c * E
                    ins = pe.matmul(bank[:, 4, t * E:(t + 1) * E], xf[:, c, PAD + t * P:PAD + (t + 1) * P], cols[:, a:a + E],
                                    start=(c == 0), stop=(c == C - 1))
            ins.then_inc(route_psum, 1)

            def expert(kind, e, chunks):
                return [w[:].rearrange("p (c n) -> p c n", c=chunks) for w in piece[order[kind, e]]]

            def up(m):
                e, i = m // IC, m % IC
                x_parts = [cut(xT, c, 0, T) for c in range(C)]
                pe.wait_ge(piece_ready, order["g", e] + 1)
                wait(pe, silu_ready, m - 1)
                project(m % 2, [cut(expert("g", e, C), c, i * P, (i + 1) * P) for c in range(C)], x_parts).then_inc(g_psum, 1)
                pe.wait_ge(piece_ready, order["u", e] + 1)
                wait(pe, gu_ready, m - 1)
                project(2 + m % 2, [cut(expert("u", e, C), c, i * P, (i + 1) * P) for c in range(C)], x_parts).then_inc(u_psum, 1)

            def down(m):
                e, i = m // IC, m % IC
                pe.wait_ge(piece_ready, order["d", e] + 1)
                pe.wait_ge(hid_ready, m + 1)
                for t in range(TT):
                    ins = project(4 + t, [tuple(h[:, t * P:(t + 1) * P] for h in hid[m % 3])],
                                  [cut(expert("d", e, IC), i, 0, D)], starts=(m == 0), stops=False)
                ins.then_inc(down_done, 1)

            up(0)
            pe.wait_ge(cw_ready, 1)
            for t in range(TT):
                ins = pe.transpose(bank[0:E, 5, t * P:(t + 1) * P], cw[:, t, :], ident[:])
            ins.then_inc(cwT_psum, 1)
            pe.wait_ge(cwT_ready, 1)
            pe.wait_ge(masks_ready, MASKS)
            for e in range(EM):
                pe.matmul(bank[:, 4 + e, :], select[:, e, :], cwT[:], start=True, stop=True).then_inc(cwB_psum, 1)
            up(1)
            pe.wait_ge(cwB_ready, EM)
            for m in range(2, M):
                up(m)
                down(m - 2)
            down(M - 2)
            down(M - 1)
            pe.wait_ge(conv_ready, C)
            for t in range(TT):
                for c in range(C):
                    ins = pe.matmul(bank[:, 4 + t, c * P:(c + 1) * P], conv[:, c, t * P:(t + 1) * P], ident[:],
                                    start=False, stop=(c == C - 1))
                ins.then_inc(o_psum, 1)


def kernel(x, ctx_1024, L0_xattn_Wq, L0_xattn_bq, L0_xattn_Wk, L0_xattn_bk, L0_xattn_Wv, L0_xattn_bv, L0_xattn_Wo,
           L0_xattn_bo, L0_attn_W_qkv, L0_attn_qn_w, L0_attn_kn_w, L0_attn_W_out, L0_attn_b_out, L0_ffn_Wr,
           L0_ffn_router_bias, L0_ffn_Wg, L0_ffn_Wu, L0_ffn_Wd, L0_ffn_conv_w, L0_ffn_conv_b):
    import numpy as np
    import concourse.bacc as bacc
    from concourse.bass_utils import run_bass_kernel_spmd

    def on_partitions(w):
        w = np.asarray(w)
        return np.ascontiguousarray(w.reshape(-1, P, w.shape[-1]).transpose(1, 0, 2))

    def column(v):
        return np.asarray(v).reshape(-1, P).T

    ctx = np.asarray(ctx_1024)[0].reshape(NB, KC, P, C, P)
    wqkv = np.asarray(L0_attn_W_qkv)
    matrices = {"g": L0_ffn_Wg, "u": L0_ffn_Wu, "d": L0_ffn_Wd}
    arrays = {
        "x": np.ascontiguousarray(np.asarray(x)[0].reshape(TT, P, D)),
        "ctx_t": np.ascontiguousarray(ctx.transpose(0, 4, 3, 1, 2).reshape(NB, P, C, KB)),
        "ctx_n": np.ascontiguousarray(ctx.transpose(0, 2, 1, 3, 4).reshape(NB, P, KC, D)),
        "wq_t": on_partitions(np.asarray(L0_xattn_Wq).T),
        "wk_in": on_partitions(L0_xattn_Wk),
        "wv_t": on_partitions(np.asarray(L0_xattn_Wv).T),
        "wo_t": on_partitions(np.asarray(L0_xattn_Wo).T),
        "wqkv_in": np.stack([on_partitions(wqkv[:, s * D:(s + 1) * D]) for s in range(3)]),
        "wout_in": on_partitions(L0_attn_W_out),
        "pieces": np.stack([on_partitions(np.asarray(matrices[kind])[e]).reshape(P, PIECE) for kind, e in PIECES]),
        "cols_in": np.ascontiguousarray(np.concatenate(
            [column(L0_xattn_bq), column(L0_xattn_bk), column(L0_xattn_bv), column(L0_attn_qn_w),
             column(L0_ffn_conv_b),
             np.asarray(L0_ffn_conv_w).reshape(TAPS, C, P).transpose(2, 1, 0).reshape(P, C * TAPS),
             on_partitions(L0_ffn_Wr).reshape(P, C * E)], axis=1)),
        "rows_in": np.concatenate([np.asarray(v).reshape(-1) for v in
                                   (L0_xattn_bo, L0_attn_kn_w, L0_attn_b_out, L0_ffn_router_bias)]),
    }
    nc = bacc.Bacc("TRN2", target_bir_lowering=False, num_devices=1)
    args = {name: nc.dram_tensor(name, a.shape, mybir.dt.from_np(a.dtype), kind="ExternalInput").ap()
            for name, a in arrays.items()}
    out = nc.dram_tensor("out", (TT, P, D), F32, kind="ExternalOutput").ap()
    perceiver_block(nc, **args, out=out)
    result = run_bass_kernel_spmd(nc, [arrays], core_ids=[0])
    return result.results[0]["out"].reshape(1, T, D)
```

```python
from contextlib import ExitStack

import concourse.bass as bass
from concourse import mybir

ALU = mybir.AluOpType
ACT = mybir.ActivationFunctionType
AX = mybir.AxisListType
F32 = mybir.dt.float32
F32R = mybir.dt.float32r

P = 128
D = 512
C = D // P
T = 512
TT = T // P
KEYS = 8192
KB = 512
NB = KEYS // KB
KC = KB // P
STEPS = NB * TT
GROUP = 2 * TT
GROUPS = STEPS // GROUP
HALF = T // 2
SCALE = float(D // 16) ** -0.5
LN_EPS = 1e-5
RMS_EPS = 1e-6
DEN_EPS = 1e-6
TOP_EPS = 1e-9
DH = 32
HG = P // DH
VW = P + HG
E = 8
EM = 4
HID = 256
IC = HID // P
M = EM * IC
TAPS = 4
WARM = 40
PAD = TAPS - 1
LOWEST = -3.0e38
ARENA = 184
PIECE = C * HID
PIECES = [("g", 0), ("u", 0), ("g", 1), ("u", 1), ("d", 0), ("g", 2), ("u", 2), ("d", 1), ("g", 3), ("u", 3),
          ("d", 2), ("d", 3)]

COLS = {}
NCOLS = 0
for _name, _n in (("bq", C), ("bk", C), ("bv", C), ("qn", C), ("conv_b", C), ("conv_w", C * TAPS), ("wr", C * E)):
    COLS[_name] = NCOLS
    NCOLS += _n
ROWS = {"bo": (0, D), "kn": (D, 2 * D), "b_out": (2 * D, 3 * D), "rb": (3 * D, 3 * D + E)}
NROWS = 3 * D + E


def perceiver_block(nc, x, ctx_t, ctx_n, wq_t, wk_in, wv_t, wo_t, wqkv_in, wout_in, pieces, cols_in, rows_in, out):
    with ExitStack() as stack:
        def sb(name, shape, dt=F32, on=stack):
            return on.enter_context(nc.sbuf_tensor(name, shape, dt))

        def sem(name):
            return stack.enter_context(nc.semaphore(name))

        bank = stack.enter_context(nc.psum_tensor("bank", [P, 8, 512], F32))

        ident = sb("ident", [P, P])
        cols = sb("cols", [P, NCOLS])
        rows = sb("rows", [P, NROWS])
        xs = sb("xs", [P, TT, D])
        xn = sb("xn", [P, TT, D])
        stats = sb("stats", [P, TT, 6])
        mv = sb("mv", [P, TT, 2])
        var = sb("var", [P, TT])
        std = sb("std", [P, TT])
        rstd = sb("rstd", [P, TT])
        shift = sb("shift", [P, TT])
        arena = sb("arena", [P, ARENA * 256])
        base = nc.sbuf_base - ARENA * 1024

        def col(name, i):
            a = COLS[name] + i
            return cols[:, a:a + 1]

        def row(name):
            a, b = ROWS[name]
            return rows[:, a:b]

        def at(kib, name, shape, dt=F32):
            size = 4
            for n in shape[1:]:
                size *= n
            assert kib * 1024 + size <= ARENA * 1024
            return nc.alloc_sbuf_tensor_at(name, shape, dt, offset=base + int(kib * 1024))

        def parts(kib, name, shape):
            size = 4
            for n in shape[1:]:
                size *= n
            return at(kib, name + "_h", shape, F32R), at(kib + size / 1024, name + "_l", shape, F32R)

        xT = parts(0, "xT", [P, C, T])
        wq = parts(16, "wq", [P, C, D])
        wk = parts(32, "wk", [P, C, D])
        wq_raw = at(144, "wq_raw", [P, C, D])
        wk_raw = at(152, "wk_raw", [P, C, D])
        qT = parts(144, "qT", [P, C, T])
        bk = parts(164, "bk", [P, C, P])
        diagonal = at(168, "diagonal", [P, TT, P])
        wv_raw = at(0, "wv_raw", [P, C, D])
        wo_raw = at(8, "wo_raw", [P, C, D])
        wv = parts(16, "wv", [P, C, D])
        wo = parts(32, "wo", [P, C, D])
        qk = parts(48, "qk", [P, C, T])
        raw_t = [at(64 + 8 * b, f"raw_t{b}", [P, C, KB]) for b in range(2)]
        raw_n = [at(80 + 8 * b, f"raw_n{b}", [P, KC, D]) for b in range(2)]
        ct = [parts(96 + 16 * b, f"ct{b}", [P, C, KB]) for b in range(2)]
        cn = [parts(128 + 16 * b, f"cn{b}", [P, KC, D]) for b in range(2)]
        probs = [at(160 + 2 * b, f"probs{b}", [P, KB]) for b in range(2)]
        pt = [parts(164 + 4 * b, f"pt{b}", [P, KC, P]) for b in range(2)]
        acc = xn
        small = at(175.5, "small", [P, 11 * TT])

        def stat(n, width=1):
            return small[:, n * TT:(n + width) * TT]

        run_max = stat(0, 2).rearrange("p (m t) -> p m t", m=2)
        block_max, neg_max, exp_bias, key_bias, alpha, row_sum, den, inv_den = (stat(n) for n in range(2, 10))
        kvmask = at(172.5, "kvmask", [P, VW])
        lower = at(173.25, "lower", [P, E, E])
        wr = parts(175.6875, "wr", [P, C, E])
        wqkv = [ct[0], cn[0], ct[1]]
        wout = cn[1]
        vT = parts(48, "vT", [P, C, T])
        square = at(48, "square", [P, D])
        qs = at(64, "qs", [P, TT, D])
        ks = at(72, "ks", [P, TT, D])
        vs = at(80, "vs", [P, TT, C, VW])
        qrT = at(160, "qrT", [P, C, T])
        kv = at(168.25, "kv", [P, C, VW])
        heads = qs
        late = at(62, "late", [P, 512])

        def late_stat(a, *dims):
            n = 1
            for d in dims:
                n *= d
            v = late[:, a:a + n]
            names = " ".join("abc"[:len(dims)])
            sizes = {"abc"[i]: dims[i] for i in range(len(dims))}
            return v.rearrange(f"p ({names}) -> p {names}", **sizes) if len(dims) > 1 else v

        ssq = late_stat(0, TT, 2)
        rms = late_stat(8, TT, 2)
        rrms = late_stat(16, TT, 2)
        norm = late_stat(32, TT, C, HG)
        rnorm = late_stat(96, TT, C, HG)
        sig = late_stat(160, TT, E)
        biased = late_stat(192, TT, E)
        rank = late_stat(224, TT, E)
        gate = late_stat(256, TT, E)
        cw = late_stat(288, TT, E)
        gsum = late_stat(320, TT)
        grec = late_stat(324, TT)
        cw_id = late_stat(328, TT)
        piece_raw = [at(176 + 4 * b, f"piece_raw{b}", [P, PIECE]) for b in range(2)]
        piece = [parts(k, f"piece{n}", [P, PIECE]) for n, k in enumerate((16, 24, 32, 40, 96, 104, 112, 120, 128, 136, 144, 152))]
        order = {(kind, e): n for n, (kind, e) in enumerate(PIECES)}
        xf = at(160, "xf", [P, C, PAD + T])
        score_rows = at(168.25, "score_rows", [E, T])
        above = at(170.25, "above", [P, TT, E, E])
        tied = at(171.25, "tied", [P, TT, E, E])
        conv = at(48, "conv", [P, C, T])
        relu_x = at(56, "relu_x", [P, 2, D])
        hid = [parts(64 + 4 * b, f"hid{b}", [P, T]) for b in range(3)]
        hid_full = [at(76 + 2 * b, f"hid_full{b}", [P, T]) for b in range(2)]
        act_g = [at(80 + 2 * b, f"act_g{b}", [P, T]) for b in range(2)]

        x_loaded = [sem(f"x_loaded{t}") for t in range(TT)]
        cols_loaded = sem("cols_loaded")
        rows_loaded = sem("rows_loaded")
        wq_loaded = [sem(f"wq_loaded{e}") for e in range(C)]
        wk_loaded = sem("wk_loaded")
        wv_loaded = sem("wv_loaded")
        wo_loaded = sem("wo_loaded")
        piece_loaded = [sem(f"piece_loaded{b}") for b in range(2)]
        piece_high = sem("piece_high")
        piece_ready = sem("piece_ready")
        wq_high = sem("wq_high")
        wq_ready = sem("wq_ready")
        wk_high = sem("wk_high")
        wk_ready = sem("wk_ready")
        wvo_high = sem("wvo_high")
        wvo_ready = sem("wvo_ready")
        raw_loaded = [sem(f"raw_loaded{b}") for b in range(2)]
        out_stored = sem("out_stored")

        ident_ready = sem("ident_ready")
        pads_ready = sem("pads_ready")
        masks_ready = sem("masks_ready")
        bo_added = sem("bo_added")
        ln_step = sem("ln_step")
        var_ready = sem("var_ready")
        std_ready = sem("std_ready")
        shift_ready = sem("shift_ready")
        xn_ready = sem("xn_ready")
        xnT_psum = sem("xnT_psum")
        xh_ready = sem("xh_ready")
        xl_ready = sem("xl_ready")
        xf_ready = sem("xf_ready")
        q_psum = sem("q_psum")
        qTh_ready = sem("qTh_ready")
        qTl_ready = sem("qTl_ready")
        bk_high = sem("bk_high")
        bk_ready = sem("bk_ready")
        acc_cleared = sem("acc_cleared")
        wr_high = sem("wr_high")
        wr_ready = sem("wr_ready")
        qk_psum = sem("qk_psum")
        qkh_ready = sem("qkh_ready")
        qkl_ready = sem("qkl_ready")
        keyb_psum = sem("keyb_psum")
        init_done = sem("init_done")

        ctxh_ready = sem("ctxh_ready")
        ctxl_ready = sem("ctxl_ready")
        s_done = sem("s_done")
        max_step = sem("max_step")
        bias_ready = sem("bias_ready")
        exp_done = sem("exp_done")
        alpha_ready = sem("alpha_ready")
        t_done = sem("t_done")
        pth_ready = sem("pth_ready")
        ptl_ready = sem("ptl_ready")
        pv_done = sem("pv_done")
        acc_done = sem("acc_done")
        den_done = sem("den_done")
        inv_ready = sem("inv_ready")

        v_psum = sem("v_psum")
        vTh_ready = sem("vTh_ready")
        vTl_ready = sem("vTl_ready")
        y_psum = sem("y_psum")
        x1_ready = sem("x1_ready")
        bout_added = sem("bout_added")
        q2_psum = sem("q2_psum")
        k2_psum = sem("k2_psum")
        v2_psum = sem("v2_psum")
        q_ssq = sem("q_ssq")
        k_ssq = sem("k_ssq")
        ms_ready = sem("ms_ready")
        rms_ready = sem("rms_ready")
        rrms_ready = sem("rrms_ready")
        qs_ready = sem("qs_ready")
        kw_ready = sem("kw_ready")
        k_ready = sem("k_ready")
        v_ready = sem("v_ready")
        qsT_psum = sem("qsT_psum")
        qrT_ready = sem("qrT_ready")
        kv_psum = sem("kv_psum")
        kv_ready = sem("kv_ready")
        la_psum = sem("la_psum")
        norm_ready = sem("norm_ready")
        rnorm_ready = sem("rnorm_ready")
        heads_ready = sem("heads_ready")
        z_psum = sem("z_psum")
        x2_ready = sem("x2_ready")
        route_psum = sem("route_psum")
        sig_ready = sem("sig_ready")
        route_step = sem("route_step")
        scoreT_psum = sem("scoreT_psum")
        cw_ready = sem("cw_ready")
        xs_added = sem("xs_added")
        relu_ready = sem("relu_ready")
        conv_step = sem("conv_step")
        conv_ready = sem("conv_ready")
        g_psum = sem("g_psum")
        u_psum = sem("u_psum")
        silu_ready = sem("silu_ready")
        hid_full_ready = sem("hid_full_ready")
        hidh_ready = sem("hidh_ready")
        hid_ready = sem("hid_ready")
        down_psum = sem("down_psum")
        conv_psum = sem("conv_psum")
        out_ready = sem("out_ready")

        def wait(eng, s, n):
            if isinstance(n, int) and n <= 0:
                return
            eng.wait_ge(s, n)

        def over_steps(eng, step):
            for i in range(GROUP):
                step(i, i)
            with eng.Fori(1, GROUPS - 1) as g:
                for u in range(GROUP):
                    step(g * GROUP + u, u)
            for u in range(GROUP):
                step(STEPS - GROUP + u, u, last=True)

        block = stack.enter_context(nc.Block())

        @block.sync
        def _(sp):
            for t in range(0, TT, 2):
                for n in range(t, t + 2):
                    sp.dma_start(xs[:, n, :], x[n]).then_inc(x_loaded[n], 16)
                for e in range(t, t + 2):
                    sp.dma_start(wq_raw[:, e, :], wq_t[e]).then_inc(wq_loaded[e], 16)
            sp.dma_start(cols[:], cols_in).then_inc(cols_loaded, 16)
            sp.dma_start(wk_raw[:], wk_in).then_inc(wk_loaded, 16)
            for b in range(2):
                sp.dma_start(raw_t[b][:], ctx_t[b]).then_inc(raw_loaded[b], 16)
                sp.dma_start(raw_n[b][:], ctx_n[b]).then_inc(raw_loaded[b], 16)
            sp.dma_start(rows[:], rows_in.partition_broadcast(P)).then_inc(rows_loaded, 16)
            sp.wait_ge(q_psum, 2 * C)
            sp.dma_start(wv_raw[:], wv_t).then_inc(wv_loaded, 16)
            sp.dma_start(wo_raw[:], wo_t).then_inc(wo_loaded, 16)
            for n in range(2):
                sp.dma_start(piece_raw[n][:], pieces[n]).then_inc(piece_loaded[n], 16)
            with sp.Fori(1, NB // 2) as g:
                for b in range(2):
                    sp.wait_ge(ctxl_ready, g * (2 * TT) + (b - 1) * TT)
                    sp.dma_start(raw_t[b][:], ctx_t[bass.ds(g * 2 + b, 1)].rearrange("a p c k -> (a p) c k")).then_inc(raw_loaded[b], 16)
                    sp.dma_start(raw_n[b][:], ctx_n[bass.ds(g * 2 + b, 1)].rearrange("a p c k -> (a p) c k")).then_inc(raw_loaded[b], 16)
            for b in range(2):
                sp.wait_ge(ctxl_ready, (NB - 1 + b) * TT)
                sp.dma_start(raw_t[b][:], wqkv_in[2 * b]).then_inc(raw_loaded[b], 16)
                sp.dma_start(raw_n[b][:], wqkv_in[1] if b == 0 else wout_in).then_inc(raw_loaded[b], 16)
            for n in range(2, len(PIECES)):
                sp.wait_ge(piece_ready, n - 1)
                sp.dma_start(piece_raw[n % 2][:], pieces[n]).then_inc(piece_loaded[n % 2], 16)
            for t in range(TT):
                sp.wait_ge(out_ready, t + 1)
                sp.dma_start(out[t], xs[:, t, :]).then_inc(out_stored, 16)
            sp.wait_ge(out_stored, 16 * TT)

        @block.gpsimd
        def _(pool):
            pool.memset(ident[:], 0.0).then_inc(ident_ready, 1)
            pool.wait_ge(ident_ready, 1)
            pool.affine_select(out=ident[:], in_=ident[:], compare_op=ALU.not_equal, fill=1.0, base=0,
                               pattern=[[-1, P]], channel_multiplier=1).then_inc(ident_ready, 1)
            for e in range(C):
                pool.wait_ge(wq_high, e + 1)
                pool.tensor_tensor(wq[1][:, e, :], wq_raw[:, e, :], wq[0][:, e, :].bitcast(F32), ALU.subtract).then_inc(wq_ready, 1)
            pool.wait_ge(wk_high, 1)
            pool.tensor_tensor(wk[1][:], wk_raw[:], wk[0][:].bitcast(F32), ALU.subtract).then_inc(wk_ready, 1)
            pool.wait_ge(bk_high, 1)
            a = COLS["bk"]
            pool.tensor_tensor(bk[1][:], cols[:, a:a + C].unsqueeze(2).to_broadcast([P, C, P]), bk[0][:].bitcast(F32),
                               ALU.subtract).then_inc(bk_ready, 1)
            a = COLS["wr"]
            pool.tensor_copy(wr[0][:].rearrange("p c e -> p (c e)"), cols[:, a:a + C * E]).then_inc(wr_high, 1)
            pool.wait_ge(wr_high, 1)
            pool.tensor_tensor(wr[1][:].rearrange("p c e -> p (c e)"), cols[:, a:a + C * E],
                               wr[0][:].rearrange("p c e -> p (c e)").bitcast(F32), ALU.subtract).then_inc(wr_ready, 1)
            pool.wait_ge(xnT_psum, TT)
            pool.memset(acc[:], 0.0).then_inc(acc_cleared, 1)
            pool.wait_ge(rows_loaded, 16)
            pool.wait_ge(xn_ready, TT)
            for t in range(TT):
                pool.tensor_tensor(xs[:, t, :], xs[:, t, :], row("bo"), ALU.add).then_inc(bo_added, 1)
            pool.wait_ge(qk_psum, 2 * C)
            for n, (raw, w, loaded) in enumerate(((wv_raw, wv, wv_loaded), (wo_raw, wo, wo_loaded))):
                pool.wait_ge(loaded, 16)
                pool.tensor_copy(w[0][:], raw[:]).then_inc(wvo_high, 1)
                pool.wait_ge(wvo_high, n + 1)
                pool.tensor_tensor(w[1][:], raw[:], w[0][:].bitcast(F32), ALU.subtract).then_inc(wvo_ready, 1)
            pool.memset(kvmask[:], 0.0).then_inc(masks_ready, 1)
            pool.memset(lower[:], 0.0).then_inc(masks_ready, 1)
            pool.wait_ge(masks_ready, 2)
            made = 2
            for h in range(HG):
                pool.memset(kvmask[h * DH:(h + 1) * DH, h * DH:(h + 1) * DH], 1.0).then_inc(masks_ready, 1)
                made += 1
                pool.wait_ge(masks_ready, made)
                pool.memset(kvmask[h * DH:(h + 1) * DH, P + h:P + h + 1], 1.0).then_inc(masks_ready, 1)
                made += 1
                pool.wait_ge(masks_ready, made)
            for e in range(1, E):
                pool.memset(lower[:, e, 0:e], 1.0).then_inc(masks_ready, 1)
                made += 1
                pool.wait_ge(masks_ready, made)
            pool.wait_ge(ctxl_ready, (NB + 2) * TT)
            pool.memset(vs[:, :, :, P:VW], 1.0).then_inc(pads_ready, 1)

            def split_piece(n):
                pool.wait_ge(piece_loaded[n % 2], 16 * (n // 2 + 1))
                pool.tensor_copy(piece[n][0][:], piece_raw[n % 2][:]).then_inc(piece_high, 1)
                pool.wait_ge(piece_high, n + 1)
                pool.tensor_tensor(piece[n][1][:], piece_raw[n % 2][:], piece[n][0][:].bitcast(F32),
                                   ALU.subtract).then_inc(piece_ready, 1)

            pool.wait_ge(y_psum, TT)
            for n in range(0, 4):
                split_piece(n)
            pool.wait_ge(xn_ready, 3 * TT)
            for t in range(TT):
                pool.tensor_tensor(xs[:, t, :], xs[:, t, :], row("b_out"), ALU.add).then_inc(bout_added, 1)
            pool.wait_ge(v2_psum, TT)
            for n in range(4, 8):
                split_piece(n)
            pool.wait_ge(la_psum, TT)
            pool.memset(xf[:, :, 0:PAD], 0.0).then_inc(pads_ready, 1)
            for n in range(8, 10):
                split_piece(n)
            pool.wait_ge(z_psum, TT)
            for n in range(10, 12):
                split_piece(n)

        def terms_with(e, t):
            return e * TT + t + 1 + 2 * min(TT, IC * (e + 1))

        XT_BANKS = (0, 1, 2, 3)
        Q_BANKS = ((4, 5, 6, 7), (0, 1, 2, 3))
        ON_BANKS = (6, 7, 0, 1)
        V_BANKS = ((2, 3, 4, 5), (6, 7, 0, 1))
        Y_BANKS = (2, 3, 4, 5)
        X1_BANKS = (6, 7, 0, 1)
        KQV_BANKS = (2, 3, 4, 5, 6, 7)
        QT_BANKS = (0, 1)
        KV_BANKS = (2, 3, 4, 5)
        LA_BANKS = (6, 0, 2, 4)
        HEAD_BANKS = (6, 7, 0, 1)
        X2_BANKS = (4, 5, 6, 7)
        MASKS = 2 + 2 * HG + E - 1

        @block.scalar
        def _(act):
            def std_of(n):
                t = n % TT
                act.wait_ge(var_ready, n + 1)
                act.activation(std[:, t:t + 1], var[:, t:t + 1], ACT.Sqrt).then_inc(std_ready, 1)

            def high_xT(n, banks):
                t = n % TT
                act.wait_ge(xnT_psum, n + 1)
                act.copy(xT[0][:, :, t * P:(t + 1) * P],
                         bank[:, banks[t], :].rearrange("p (c t) -> p c t", c=C)).then_inc(xh_ready, 1)

            def apply_of(n):
                t = n % TT
                act.wait_ge(shift_ready, n + 1)
                act.activation(xn[:, t, :], xs[:, t, :], ACT.Identity, bias=shift[:, t:t + 1],
                               scale=rstd[:, t:t + 1]).then_inc(xn_ready, 1)

            def high_wq(e):
                act.wait_ge(wq_loaded[e], 16)
                act.copy(wq[0][:, e, :], wq_raw[:, e, :]).then_inc(wq_high, 1)

            for t in range(TT):
                std_of(t)
                apply_of(t)
                if t >= 1:
                    high_xT(t - 1, XT_BANKS)
                    high_wq(t - 1)
            high_xT(TT - 1, XT_BANKS)
            high_wq(TT - 1)
            act.wait_ge(wk_loaded, 16)
            act.copy(wk[0][:], wk_raw[:]).then_inc(wk_high, 1)
            act.wait_ge(cols_loaded, 16)
            a = COLS["bk"]
            act.copy(bk[0][:], cols[:, a:a + C].unsqueeze(2).to_broadcast([P, C, P])).then_inc(bk_high, 1)

            act.wait_ge(raw_loaded[0], 32)
            for u in range(TT):
                src, dst = (raw_t[0], ct[0][0]) if u < 2 else (raw_n[0], cn[0][0])
                v = 2 * (u % 2)
                act.copy(dst[:, v:v + 2, :], src[:, v:v + 2, :]).then_inc(ctxh_ready, 1)
            act.wait_ge(cols_loaded, 16)
            act.wait_ge(wq_ready, C)
            act.wait_ge(wk_ready, 1)
            for n in range(2 * C):
                c, h = n % C, n // C * HALF
                act.wait_ge(q_psum, n + 1)
                act.activation(qT[0][:, c, h:h + HALF], bank[:, Q_BANKS[n // C][c], h:h + HALF], ACT.Identity,
                               bias=col("bq", c)).then_inc(qTh_ready, 1)
            for n in range(2 * C):
                c, h = n % C, n // C * HALF
                act.wait_ge(qk_psum, n + 1)
                act.copy(qk[0][:, c, h:h + HALF], bank[:, Q_BANKS[n // C][c], h:h + HALF]).then_inc(qkh_ready, 1)

            def step(i, u, last=False):
                if not (isinstance(i, int) and i == 0):
                    b = (u - 1) % 2
                    wait(act, t_done, i)
                    wait(act, pv_done, i - 2)
                    act.copy(pt[b][0][:], bank[:, 2 + b, :].rearrange("p (c k) -> p c k", c=KC)).then_inc(pth_ready, 1)
                if isinstance(i, int) and i >= STEPS:
                    return
                t, b, m = u % TT, u % 2, (u // TT) % 2
                act.wait_ge(bias_ready, i + 1)
                act.activation(probs[b][:], bank[:, b, :], ACT.Exp, bias=exp_bias[:, t:t + 1], scale=SCALE,
                               accum_out=row_sum[:, t:t + 1]).then_inc(exp_done, 1)
                act.activation(alpha[:, t:t + 1], run_max[:, m, t:t + 1], ACT.Exp, bias=neg_max[:, t:t + 1],
                               scale=SCALE).then_inc(alpha_ready, 1)
                next_high(i, t, 1 - m)

            def next_high(i, t, nb):
                if t == 0:
                    act.wait_ge(raw_loaded[nb], (i + TT - nb * TT) * 4 + 32)
                if t < 2:
                    wait(act, s_done, i - t)
                    act.copy(ct[nb][0][:, 2 * t:2 * t + 2, :], raw_t[nb][:, 2 * t:2 * t + 2, :]).then_inc(ctxh_ready, 1)
                else:
                    v = 2 * (t - 2)
                    wait(act, pv_done, i - t)
                    act.copy(cn[nb][0][:, v:v + 2, :], raw_n[nb][:, v:v + 2, :]).then_inc(ctxh_ready, 1)

            over_steps(act, step)
            step(STEPS, 0, last=True)

            act.wait_ge(wvo_ready, 2)
            high_xT(TT + 0, ON_BANKS)
            high_xT(TT + 1, ON_BANKS)
            next_high(STEPS, 0, 1)
            high_xT(TT + 2, ON_BANKS)
            high_xT(TT + 3, ON_BANKS)
            next_high(STEPS + 1, 1, 1)
            for n in range(2 * C):
                c, h = n % C, n // C * HALF
                act.wait_ge(v_psum, n + 1)
                act.activation(vT[0][:, c, h:h + HALF], bank[:, V_BANKS[n // C][c], h:h + HALF], ACT.Identity,
                               bias=col("bv", c)).then_inc(vTh_ready, 1)
            next_high(STEPS + 2, 2, 1)
            next_high(STEPS + 3, 3, 1)
            for t in range(TT):
                std_of(TT + t)
                apply_of(TT + t)
                if t >= 2:
                    high_xT(2 * TT + t - 2, X1_BANKS)
            act.wait_ge(ctxl_ready, (NB + 2) * TT)

            def root(t, s):
                act.wait_ge(ms_ready, 2 * t + s + 1)
                act.activation(rms[:, t, s:s + 1], rms[:, t, s:s + 1], ACT.Sqrt).then_inc(rms_ready, 1)

            def square_of(t, s, done):
                act.wait_ge(done, t + 1)
                wait(act, q_ssq, 2 * t + s)
                act.activation(square[:], bank[:, KQV_BANKS[(3 * t + s) % 6], :], ACT.Square,
                               accum_out=ssq[:, t, s:s + 1]).then_inc(q_ssq, 1)
                root(t, s)

            def queries(t):
                act.wait_ge(qsT_psum, t + 1)
                for c in range(C):
                    ins = act.activation(qrT[:, c, t * P:(t + 1) * P], bank[:, QT_BANKS[t % 2], c * P:(c + 1) * P],
                                         ACT.Relu, scale=col("qn", c))
                ins.then_inc(qrT_ready, 1)

            for t in range(TT):
                square_of(t, 0, k2_psum)
                square_of(t, 1, q2_psum)
                act.wait_ge(rrms_ready, 2 * t + 2)
                act.activation(qs[:, t, :], bank[:, KQV_BANKS[(3 * t + 1) % 6], :], ACT.Copy,
                               scale=rrms[:, t, 1:2]).then_inc(qs_ready, 1)
                act.wait_ge(v2_psum, t + 1)
                act.copy(vs[:, t, :, 0:P],
                         bank[:, KQV_BANKS[(3 * t + 2) % 6], :].rearrange("p (c k) -> p c k", c=C)).then_inc(v_ready, 1)
                if t < 2:
                    high_xT(2 * TT + t + 2, X1_BANKS)
                if t >= 1:
                    queries(t - 1)
            queries(TT - 1)
            for t in range(TT):
                high_xT(3 * TT + t, HEAD_BANKS)

            def whole_xT(t):
                act.wait_ge(xl_ready, 4 * TT + t + 1)
                act.copy(xf[:, :, PAD + t * P:PAD + (t + 1) * P],
                         bank[:, X2_BANKS[t], :].rearrange("p (c t) -> p c t", c=C)).then_inc(xf_ready, 1)

            for t in range(TT):
                if t == 2:
                    high_xT(4 * TT + 0, X2_BANKS)
                    high_xT(4 * TT + 1, X2_BANKS)
                if t == 3:
                    whole_xT(0)
                    whole_xT(1)
                    high_xT(4 * TT + 2, X2_BANKS)
                std_of(2 * TT + t)
                apply_of(2 * TT + t)
            whole_xT(2)
            high_xT(4 * TT + 3, X2_BANKS)
            whole_xT(3)

            def high_hid(m):
                act.wait_ge(hid_full_ready, m + 1)
                wait(act, down_psum, (m - 2) * TT)
                act.copy(hid[m % 3][0][:], hid_full[m % 2][:]).then_inc(hidh_ready, 1)

            act.wait_ge(route_psum, 2)
            act.activation(score_rows[:], bank[0:E, 4, :], ACT.Sigmoid).then_inc(sig_ready, 1)
            for m in range(M):
                act.wait_ge(g_psum, m + 1)
                wait(act, hid_full_ready, m - 1)
                act.activation(act_g[m % 2][:], bank[:, m % 2, :], ACT.Silu).then_inc(silu_ready, 1)
                if m >= 1:
                    high_hid(m - 1)
                if 2 <= m < 2 + TT:
                    t = m - 2
                    act.wait_ge(cw_ready, 1)
                    wait(act, xs_added, 2 * (t - 1))
                    act.activation(relu_x[:, t % 2, :], xn[:, t, :], ACT.Relu, scale=cw[:, t, 7:8]).then_inc(relu_ready, 1)
            high_hid(M - 1)

        @block.vector
        def _(dve):
            lnc = [0]

            def ln_chain(ins):
                ins.then_inc(ln_step, 1)
                lnc[0] += 1
                dve.wait_ge(ln_step, lnc[0])

            def ln_stats(n):
                t = n % TT
                ln_chain(dve.bn_stats(stats[:, t, :], xs[:, t, :]))
                ln_chain(dve.bn_aggr(mv[:, t, :], stats[:, t, :]))
                dve.tensor_scalar(var[:, t:t + 1], mv[:, t, 1:2], LN_EPS, None, ALU.add).then_inc(var_ready, 1)

            def ln_scale(n):
                t = n % TT
                dve.wait_ge(std_ready, n + 1)
                ln_chain(dve.reciprocal(rstd[:, t:t + 1], std[:, t:t + 1]))
                dve.tensor_scalar(shift[:, t:t + 1], mv[:, t, 0:1], rstd[:, t:t + 1], -1.0, ALU.mult,
                                  ALU.mult).then_inc(shift_ready, 1)

            def low_xT(n, banks):
                t = n % TT
                dve.wait_ge(xh_ready, n + 1)
                dve.tensor_tensor(xT[1][:, :, t * P:(t + 1) * P],
                                  bank[:, banks[t], :].rearrange("p (c t) -> p c t", c=C),
                                  xT[0][:, :, t * P:(t + 1) * P].bitcast(F32), ALU.subtract).then_inc(xl_ready, 1)

            for t in range(TT):
                dve.wait_ge(x_loaded[t], 16)
                ln_stats(t)
                ln_scale(t)
                if t:
                    low_xT(t - 1, XT_BANKS)
            low_xT(TT - 1, XT_BANKS)

            def split_low(t, b, q):
                dve.wait_ge(ctxh_ready, q + 1)
                raw, split = (raw_t, ct) if t < 2 else (raw_n, cn)
                v = 2 * (t % 2)
                dve.tensor_tensor(split[b][1][:, v:v + 2, :], raw[b][:, v:v + 2, :],
                                  split[b][0][:, v:v + 2, :].bitcast(F32),
                                  ALU.subtract).then_inc(ctxl_ready, 1)

            for t in range(TT - 1):
                split_low(t, 0, t)
            dve.wait_ge(cols_loaded, 16)
            for n in range(2 * C):
                c, h = n % C, n // C * HALF
                dve.wait_ge(qTh_ready, n + 1)
                dve.scalar_tensor_tensor(out=qT[1][:, c, h:h + HALF], in0=bank[:, Q_BANKS[n // C][c], h:h + HALF], scalar=col("bq", c),
                                         in1=qT[0][:, c, h:h + HALF].bitcast(F32), op0=ALU.add,
                                         op1=ALU.subtract).then_inc(qTl_ready, 1)
            dve.memset(run_max[:, 0, :], LOWEST).then_inc(init_done, 1)
            dve.memset(den[:], 0.0).then_inc(init_done, 1)
            for n in range(2 * C):
                c, h = n % C, n // C * HALF
                dve.wait_ge(qkh_ready, n + 1)
                dve.tensor_tensor(qk[1][:, c, h:h + HALF], bank[:, Q_BANKS[n // C][c], h:h + HALF], qk[0][:, c, h:h + HALF].bitcast(F32),
                                  ALU.subtract).then_inc(qkl_ready, 1)
            dve.wait_ge(keyb_psum, 1)
            dve.wait_ge(ident_ready, 2)
            dve.tensor_tensor(diagonal[:], bank[:, 4, :].rearrange("p (t k) -> p t k", t=TT),
                              ident[:].unsqueeze(1).to_broadcast([P, TT, P]), ALU.mult).then_inc(init_done, 1)
            dve.wait_ge(init_done, 3)
            dve.reduce_sum(key_bias[:], diagonal[:], AX.X).then_inc(init_done, 1)
            dve.wait_ge(init_done, 4)
            dve.wait_ge(acc_cleared, 1)

            def step(i, u, last=False):
                if not (isinstance(i, int) and i < 3):
                    t, b = (u - 3) % TT, (u - 3) % 2
                    dve.wait_ge(pv_done, i - 2)
                    dve.wait_ge(alpha_ready, i - 2)
                    wait(dve, den_done, i - 3)
                    dve.scalar_tensor_tensor(out=acc[:, t, :], in0=acc[:, t, :], scalar=alpha[:, t:t + 1],
                                             in1=bank[:, 4 + b, :], op0=ALU.mult, op1=ALU.add).then_inc(acc_done, 1)
                    dve.scalar_tensor_tensor(out=den[:, t:t + 1], in0=den[:, t:t + 1], scalar=alpha[:, t:t + 1],
                                             in1=row_sum[:, t:t + 1], op0=ALU.mult, op1=ALU.add).then_inc(den_done, 1)
                    if last and i - 3 >= STEPS - TT:
                        dve.wait_ge(den_done, i - 2)
                        dve.reciprocal(inv_den[:, t:t + 1], den[:, t:t + 1]).then_inc(inv_ready, 1)
                        dve.wait_ge(inv_ready, t + 1)
                        dve.tensor_scalar(acc[:, t, :], acc[:, t, :], inv_den[:, t:t + 1], None, ALU.mult).then_inc(xn_ready, 1)
                live = not (isinstance(i, int) and i >= STEPS)
                t, b, m = u % TT, u % 2, (u // TT) % 2
                if live:
                    split_low((t - 1) % TT, m if t == 0 else 1 - m, i + 3)
                if live:
                    dve.wait_ge(s_done, i + 1)
                    dve.reduce_max(block_max[:, t:t + 1], bank[:, b, :], AX.X).then_inc(max_step, 1)
                    dve.wait_ge(max_step, i * 2 + 1)
                    dve.tensor_scalar(run_max[:, 1 - m, t:t + 1], block_max[:, t:t + 1], key_bias[:, t:t + 1],
                                      run_max[:, m, t:t + 1], ALU.add, ALU.max).then_inc(max_step, 1)
                    dve.wait_ge(max_step, i * 2 + 2)
                    dve.tensor_scalar(neg_max[:, t:t + 1], run_max[:, 1 - m, t:t + 1], -SCALE, None, ALU.mult)
                    dve.tensor_scalar(exp_bias[:, t:t + 1], run_max[:, 1 - m, t:t + 1], key_bias[:, t:t + 1], -SCALE,
                                      ALU.subtract, ALU.mult).then_inc(bias_ready, 1)
                if not (isinstance(i, int) and (i == 0 or i > STEPS)):
                    b = (u - 1) % 2
                    dve.wait_ge(pth_ready, i)
                    dve.tensor_tensor(pt[b][1][:], bank[:, 2 + b, :].rearrange("p (c k) -> p c k", c=KC),
                                      pt[b][0][:].bitcast(F32), ALU.subtract).then_inc(ptl_ready, 1)

            over_steps(dve, step)
            step(STEPS, 0, last=True)
            low_xT(TT + 0, ON_BANKS)
            split_low(TT - 1, 0, STEPS + TT - 1)
            step(STEPS + 1, 1, last=True)
            low_xT(TT + 1, ON_BANKS)
            step(STEPS + 2, 2, last=True)
            low_xT(TT + 2, ON_BANKS)
            split_low(0, 1, STEPS + TT)
            low_xT(TT + 3, ON_BANKS)
            for n in range(2 * C):
                c, h = n % C, n // C * HALF
                dve.wait_ge(vTh_ready, n + 1)
                dve.scalar_tensor_tensor(out=vT[1][:, c, h:h + HALF], in0=bank[:, V_BANKS[n // C][c], h:h + HALF],
                                         scalar=col("bv", c), in1=vT[0][:, c, h:h + HALF].bitcast(F32), op0=ALU.add,
                                         op1=ALU.subtract).then_inc(vTl_ready, 1)
                if n == C - 1:
                    split_low(1, 1, STEPS + TT + 1)
            split_low(2, 1, STEPS + TT + 2)
            split_low(3, 1, STEPS + TT + 3)
            dve.wait_ge(bo_added, TT)
            for t in range(TT):
                dve.wait_ge(y_psum, t + 1)
                dve.tensor_tensor(xs[:, t, :], xs[:, t, :], bank[:, Y_BANKS[t], :], ALU.add).then_inc(x1_ready, 1)
                dve.wait_ge(x1_ready, t + 1)
                ln_stats(TT + t)
                ln_scale(TT + t)
                if t >= 2:
                    low_xT(2 * TT + t - 2, X1_BANKS)

            def over_rms(t, s):
                n = 2 * t + s
                dve.wait_ge(q_ssq, n + 1)
                dve.tensor_scalar(rms[:, t, s:s + 1], ssq[:, t, s:s + 1], 1.0 / D, RMS_EPS, ALU.mult,
                                  ALU.add).then_inc(ms_ready, 1)
                dve.wait_ge(rms_ready, n + 1)
                dve.reciprocal(rrms[:, t, s:s + 1], rms[:, t, s:s + 1]).then_inc(rrms_ready, 1)

            for t in range(TT):
                over_rms(t, 0)
                dve.wait_ge(rrms_ready, 2 * t + 1)
                dve.scalar_tensor_tensor(out=ks[:, t, :], in0=bank[:, KQV_BANKS[3 * t % 6], :], scalar=rrms[:, t, 0:1],
                                         in1=row("kn"), op0=ALU.mult, op1=ALU.mult).then_inc(kw_ready, 1)
                dve.wait_ge(kw_ready, t + 1)
                dve.tensor_scalar(ks[:, t, :], ks[:, t, :], 0.0, None, ALU.max).then_inc(k_ready, 1)
                over_rms(t, 1)
                if t < 2:
                    low_xT(2 * TT + t + 2, X1_BANKS)
            dve.wait_ge(masks_ready, MASKS)
            for c in range(C):
                dve.wait_ge(kv_psum, c + 1)
                dve.tensor_tensor(kv[:, c, :], bank[:, KV_BANKS[c], 0:VW], kvmask[:], ALU.mult).then_inc(kv_ready, 1)
            for t in range(TT):
                dve.wait_ge(la_psum, t + 1)
                la = bank[:, LA_BANKS[t]:LA_BANKS[t] + 2, 0:2 * VW].rearrange("p b (g w) -> p b g w", g=2)
                dve.tensor_scalar(norm[:, t].rearrange("p (b g) h -> p b g h", b=2), la[:, :, :, P:VW], DEN_EPS, None,
                                  ALU.add).then_inc(norm_ready, 1)
                dve.wait_ge(norm_ready, t + 1)
                dve.reciprocal(rnorm[:, t], norm[:, t]).then_inc(rnorm_ready, 1)
                dve.wait_ge(rnorm_ready, t + 1)
                for b in range(2):
                    ins = dve.tensor_tensor(
                        heads[:, t, b * 2 * P:(b + 1) * 2 * P].rearrange("p (g h e) -> p g h e", g=2, h=HG),
                        la[:, b, :, 0:P].rearrange("p g (h e) -> p g h e", h=HG),
                        rnorm[:, t, 2 * b:2 * b + 2, :].unsqueeze(3).to_broadcast([P, 2, HG, DH]), ALU.mult)
                ins.then_inc(heads_ready, 1)
                if t >= 1:
                    low_xT(3 * TT + t - 1, HEAD_BANKS)
            low_xT(4 * TT - 1, HEAD_BANKS)
            for t in range(TT):
                dve.wait_ge(z_psum, t + 1)
                dve.wait_ge(bout_added, t + 1)
                dve.tensor_tensor(xs[:, t, :], xs[:, t, :], bank[:, HEAD_BANKS[t], :], ALU.add).then_inc(x2_ready, 1)
                dve.wait_ge(x2_ready, t + 1)
                ln_stats(2 * TT + t)
                ln_scale(2 * TT + t)
                if t == 2:
                    low_xT(4 * TT, X2_BANKS)
                    low_xT(4 * TT + 1, X2_BANKS)
            low_xT(4 * TT + 2, X2_BANKS)
            low_xT(4 * TT + 3, X2_BANKS)

            rc = [0]

            def route(ins):
                ins.then_inc(route_step, 1)
                rc[0] += 1
                dve.wait_ge(route_step, rc[0])

            def router():
                dve.wait_ge(scoreT_psum, 1)
                scores = bank[:, 5, 0:TT * E].rearrange("p (t e) -> p t e", t=TT)
                dve.tensor_copy(sig[:], scores)
                route(dve.tensor_tensor(biased[:], scores, row("rb").unsqueeze(1).to_broadcast([P, TT, E]), ALU.add))
                for t in range(TT):
                    mine = biased[:, t, :].unsqueeze(2).to_broadcast([P, E, E])
                    others = biased[:, t, :].unsqueeze(1).to_broadcast([P, E, E])
                    dve.tensor_tensor(above[:, t], others, mine, ALU.is_gt)
                    ins = dve.tensor_tensor(tied[:, t], others, mine, ALU.is_equal)
                route(ins)
                route(dve.tensor_tensor(tied[:], tied[:], lower[:].unsqueeze(1).to_broadcast([P, TT, E, E]), ALU.mult))
                route(dve.tensor_tensor(above[:], above[:], tied[:], ALU.add))
                route(dve.reduce_sum(rank[:], above[:], AX.X))
                route(dve.scalar_tensor_tensor(out=gate[:], in0=rank[:], scalar=1.5, in1=sig[:], op0=ALU.is_lt, op1=ALU.mult))
                route(dve.reduce_sum(gsum[:], gate[:], AX.X))
                route(dve.tensor_scalar(gsum[:], gsum[:], TOP_EPS, None, ALU.add))
                route(dve.reciprocal(grec[:], gsum[:]))
                dve.tensor_tensor(cw[:], gate[:], grec[:].unsqueeze(2).to_broadcast([P, TT, E]), ALU.mult).then_inc(cw_ready, 1)
                dve.wait_ge(cw_ready, 1)
                route(dve.tensor_tensor(cw_id[:], cw[:, :, 4], cw[:, :, 6], ALU.add))

            def experts(m):
                dve.wait_ge(silu_ready, m + 1)
                dve.wait_ge(u_psum, m + 1)
                wait(dve, hid_ready, m - 1)
                dve.tensor_tensor(hid_full[m % 2][:], act_g[m % 2][:], bank[:, 2 + m % 2, :], ALU.mult).then_inc(hid_full_ready, 1)

            def low_hid(m):
                dve.wait_ge(hidh_ready, m + 1)
                dve.tensor_tensor(hid[m % 3][1][:], hid_full[m % 2][:], hid[m % 3][0][:].bitcast(F32),
                                  ALU.subtract).then_inc(hid_ready, 1)

            terms = [0]
            last_term = [0] * TT

            def add_term(t, in0, scalar):
                wait(dve, xs_added, last_term[t])
                if scalar is None:
                    ins = dve.tensor_tensor(xs[:, t, :], xs[:, t, :], in0, ALU.add)
                else:
                    ins = dve.scalar_tensor_tensor(out=xs[:, t, :], in0=in0, scalar=scalar, in1=xs[:, t, :],
                                                   op0=ALU.mult, op1=ALU.add)
                ins.then_inc(xs_added, 1)
                terms[0] += 1
                last_term[t] = terms[0]

            def add_expert(e):
                for t in range(TT):
                    dve.wait_ge(down_psum, (e * IC + IC - 1) * TT + t + 1)
                    add_term(t, bank[:, 4 + t, :], cw[:, t, e:e + 1])

            convc = [0]

            def conv_chain(ins):
                ins.then_inc(conv_step, 1)
                convc[0] += 1
                dve.wait_ge(conv_step, convc[0])

            dve.wait_ge(pads_ready, 2)
            dve.wait_ge(xf_ready, TT)
            for m in range(M):
                if m >= 4 and m % IC == 0:
                    add_expert(m // IC - 2)
                experts(m)
                if m >= 1:
                    low_hid(m - 1)
                if m == 1:
                    router()
                if 2 <= m < 2 + TT:
                    t = m - 2
                    add_term(t, xn[:, t, :], cw_id[:, t:t + 1])
                    dve.wait_ge(relu_ready, t + 1)
                    add_term(t, relu_x[:, t % 2, :], None)
                if 2 <= m < 2 + C:
                    c = m - 2

                    def tap(j):
                        return cols[:, COLS["conv_w"] + c * TAPS + j:COLS["conv_w"] + c * TAPS + j + 1]

                    conv_chain(dve.tensor_scalar(conv[:, c, :], xf[:, c, 0:T], tap(0), col("conv_b", c), ALU.mult, ALU.add))
                    for j in range(1, TAPS):
                        ins = dve.scalar_tensor_tensor(out=conv[:, c, :], in0=xf[:, c, j:j + T], scalar=tap(j),
                                                       in1=conv[:, c, :], op0=ALU.mult, op1=ALU.add)
                        if j < TAPS - 1:
                            conv_chain(ins)
                    ins.then_inc(conv_ready, 1)
            low_hid(M - 1)
            add_expert(EM - 2)
            for t in range(TT):
                dve.wait_ge(conv_psum, t + 1)
                add_term(t, bank[:, t, :], None)
            for t in range(TT):
                dve.wait_ge(down_psum, (M - 1) * TT + t + 1)
                wait(dve, xs_added, last_term[t])
                dve.scalar_tensor_tensor(out=xs[:, t, :], in0=bank[:, 4 + t, :], scalar=cw[:, t, EM - 1:EM],
                                         in1=xs[:, t, :], op0=ALU.mult, op1=ALU.add).then_inc(out_ready, 1)

        @block.tensor
        def _(pe):
            def transpose_tile(src, t, dst):
                for c in range(C):
                    ins = pe.transpose(bank[:, dst, c * P:(c + 1) * P], src[:, t, c * P:(c + 1) * P], ident[:])
                return ins

            def project(dst, lhs, rhs, starts=True, stops=True, cols=slice(0, 512), rows=slice(0, P)):
                n = len(lhs)
                for c in range(n):
                    (a_h, a_l), (b_h, b_l) = lhs[c], rhs[c]
                    for k, (a, b) in enumerate(((a_h, b_h), (a_h, b_l), (a_l, b_h))):
                        ins = pe.matmul(bank[rows, dst, cols], a, b, start=(starts and c == 0 and k == 0),
                                        stop=(stops and c == n - 1 and k == 2))
                return ins

            def cut(w, c, a, b):
                return w[0][:, c, a:b], w[1][:, c, a:b]

            pe.wait_ge(ident_ready, 2)
            for n in range(WARM):
                pe.matmul(bank[:, 7, 0:P], ident[:], ident[:], start=True, stop=True)

            def transpose_x(t):
                pe.wait_ge(xn_ready, t + 1)
                transpose_tile(xn, t, XT_BANKS[t]).then_inc(xnT_psum, 1)

            def q_half(h, e):
                pe.wait_ge(xl_ready, 2 * (h + 1))
                pe.wait_ge(wq_ready, e + 1)
                part = slice(h * HALF, (h + 1) * HALF)
                project(Q_BANKS[h][e], [cut(wq, e, c * P, (c + 1) * P) for c in range(C)],
                        [cut(xT, c, part.start, part.stop) for c in range(C)], cols=part).then_inc(q_psum, 1)

            transpose_x(0)
            transpose_x(1)
            q_half(0, 0)
            transpose_x(2)
            q_half(0, 1)
            transpose_x(3)
            q_half(0, 2)
            q_half(0, 3)
            for e in range(C):
                q_half(1, e)
            pe.wait_ge(wk_ready, 1)
            for h in range(2):
                pe.wait_ge(qTl_ready, (h + 1) * C)
                part = slice(h * HALF, (h + 1) * HALF)
                for c in range(C):
                    project(Q_BANKS[h][c], [cut(wk, e, c * P, (c + 1) * P) for e in range(C)],
                            [cut(qT, e, part.start, part.stop) for e in range(C)], cols=part).then_inc(qk_psum, 1)
            pe.wait_ge(bk_ready, 1)
            pe.wait_ge(qkl_ready, C)
            project(4, [cut(bk, e, 0, P) for e in range(C)], [cut(qT, e, 0, T) for e in range(C)]).then_inc(keyb_psum, 1)
            pe.wait_ge(qkl_ready, 2 * C)

            def scores(i, u):
                t, b, m = u % TT, u % 2, (u // TT) % 2
                if t == 0:
                    pe.wait_ge(ctxl_ready, i + 2)
                wait(pe, exp_done, i - 1)
                ins = project(b, [cut(qk, c, t * P, (t + 1) * P) for c in range(C)],
                              [cut(ct[m], c, 0, KB) for c in range(C)])
                ins.then_inc(s_done, 1)

            def transposes(i, u):
                b = u % 2
                pe.wait_ge(exp_done, i + 1)
                wait(pe, ptl_ready, i - 1)
                for c in range(KC):
                    ins = pe.transpose(bank[:, 2 + b, c * P:(c + 1) * P], probs[b][:, c * P:(c + 1) * P], ident[:])
                ins.then_inc(t_done, 1)

            def weighted_sums(i, u):
                t, b, m = u % TT, u % 2, (u // TT) % 2
                pe.wait_ge(ptl_ready, i + 1)
                if t == 0:
                    pe.wait_ge(ctxl_ready, i + 4)
                wait(pe, acc_done, i - 1)
                ins = project(4 + b, [cut(pt[b], c, 0, P) for c in range(KC)],
                              [cut(cn[m], c, 0, D) for c in range(KC)])
                ins.then_inc(pv_done, 1)

            def step(i, u, last=False):
                if not (isinstance(i, int) and i >= STEPS):
                    scores(i, u)
                if not (isinstance(i, int) and (i < 1 or i > STEPS)):
                    transposes(i - 1, (u - 1) % GROUP)
                if not (isinstance(i, int) and i < 2):
                    weighted_sums(i - 2, (u - 2) % GROUP)

            over_steps(pe, step)

            def transpose_output(t):
                pe.wait_ge(xn_ready, TT + t + 1)
                transpose_tile(acc, t, ON_BANKS[t]).then_inc(xnT_psum, 1)

            def v_half(h, e):
                pe.wait_ge(xl_ready, TT + 2 * (h + 1))
                part = slice(h * HALF, (h + 1) * HALF)
                project(V_BANKS[h][e], [cut(wv, c, e * P, (e + 1) * P) for c in range(C)],
                        [cut(xT, c, part.start, part.stop) for c in range(C)], cols=part).then_inc(v_psum, 1)

            transposes(STEPS - 1, GROUP - 1)
            transpose_output(0)
            weighted_sums(STEPS - 2, GROUP - 2)
            transpose_output(1)
            weighted_sums(STEPS - 1, GROUP - 1)
            transpose_output(2)
            pe.wait_ge(ptl_ready, STEPS)
            v_half(0, 0)
            v_half(0, 1)
            transpose_output(3)
            pe.wait_ge(acc_done, STEPS)
            v_half(0, 2)
            v_half(0, 3)
            for e in range(C):
                v_half(1, e)

            def transpose_x1(t):
                pe.wait_ge(xn_ready, 2 * TT + t + 1)
                transpose_tile(xn, t, X1_BANKS[t]).then_inc(xnT_psum, 1)

            for t in range(TT):
                pe.wait_ge(vTl_ready, (t // 2 + 1) * C)
                if t == TT - 1:
                    transpose_x1(0)
                project(Y_BANKS[t], [cut(vT, e, t * P, (t + 1) * P) for e in range(C)],
                        [cut(wo, e, 0, D) for e in range(C)]).then_inc(y_psum, 1)
            transpose_x1(1)

            def transpose_q(t):
                pe.wait_ge(qs_ready, t + 1)
                wait(pe, qrT_ready, t - 1)
                for c in range(C):
                    ins = pe.transpose(bank[:, QT_BANKS[t % 2], c * P:(c + 1) * P], qs[:, t, c * P:(c + 1) * P], ident[:])
                ins.then_inc(qsT_psum, 1)

            pe.wait_ge(ctxl_ready, (NB + 2) * TT)
            for t in range(TT):
                pe.wait_ge(xl_ready, 2 * TT + t + 1)
                for s, (w, done) in enumerate(((wqkv[1], k2_psum), (wqkv[0], q2_psum), (wqkv[2], v2_psum))):
                    n = 3 * t + s
                    if n < 4:
                        pe.wait_ge(x1_ready, n + 1)
                    elif n < 6:
                        pe.wait_ge(xl_ready, 2 * TT + n - 3)
                    if n >= 6:
                        pe.wait_ge((kw_ready, qs_ready, v_ready)[s], t - 1)
                    project(KQV_BANKS[n % 6], [cut(xT, c, t * P, (t + 1) * P) for c in range(C)],
                            [cut(w, c, 0, D) for c in range(C)]).then_inc(done, 1)
                if t < 2:
                    transpose_x1(t + 2)
                if t >= 1:
                    if t == 1:
                        pe.wait_ge(xl_ready, 3 * TT - 1)
                    if t == 2:
                        pe.wait_ge(xl_ready, 3 * TT)
                    transpose_q(t - 1)
            transpose_q(TT - 1)
            pe.wait_ge(kw_ready, TT)
            pe.wait_ge(v_ready, TT)
            pe.wait_ge(k_ready, TT)
            pe.wait_ge(pads_ready, 1)
            for c in range(C):
                for t in range(TT):
                    ins = pe.matmul(bank[:, KV_BANKS[c], 0:VW], ks[:, t, c * P:(c + 1) * P], vs[:, t, c, :],
                                    start=(t == 0), stop=(t == TT - 1))
                ins.then_inc(kv_psum, 1)
            pe.wait_ge(kv_ready, C)
            pe.wait_ge(qrT_ready, C)
            for t in range(TT):
                for c in range(C):
                    ins = pe.matmul(bank[:, LA_BANKS[t] + c // 2, c % 2 * VW:(c % 2 + 1) * VW],
                                    qrT[:, c, t * P:(t + 1) * P], kv[:, c, :], start=True, stop=True)
                ins.then_inc(la_psum, 1)

            def transpose_heads(t):
                pe.wait_ge(heads_ready, t + 1)
                transpose_tile(heads, t, HEAD_BANKS[t]).then_inc(xnT_psum, 1)

            def transpose_x2(t):
                pe.wait_ge(xn_ready, 3 * TT + t + 1)
                transpose_tile(xn, t, X2_BANKS[t]).then_inc(xnT_psum, 1)

            transpose_heads(0)
            transpose_heads(1)
            for t in range(TT):
                pe.wait_ge(xl_ready, 3 * TT + t + 1)
                if t == TT - 1:
                    transpose_x2(0)
                    transpose_x2(1)
                project(HEAD_BANKS[t], [cut(xT, c, t * P, (t + 1) * P) for c in range(C)],
                        [cut(wout, c, 0, D) for c in range(C)]).then_inc(z_psum, 1)
                if t < 2:
                    transpose_heads(t + 2)

            def route_half(h):
                pe.wait_ge(xf_ready, 1)
                pe.wait_ge(xl_ready, 4 * TT + 2 * (h + 1))
                pe.wait_ge(wr_ready, 1)
                part = slice(h * HALF, (h + 1) * HALF)
                project(4, [cut(wr, c, 0, E) for c in range(C)], [cut(xT, c, part.start, part.stop) for c in range(C)],
                        cols=part, rows=slice(0, E)).then_inc(route_psum, 1)

            def expert(kind, e, chunks):
                return [w[:].rearrange("p (c n) -> p c n", c=chunks) for w in piece[order[kind, e]]]

            def up(m, part=slice(0, T)):
                e, i = m // IC, m % IC
                pe.wait_ge(xl_ready, 4 * TT + part.stop // P)
                x_parts = [cut(xT, c, part.start, part.stop) for c in range(C)]
                pe.wait_ge(piece_ready, order["g", e] + 1)
                wait(pe, silu_ready, m - 1)
                gates = project(m % 2, [cut(expert("g", e, C), c, i * P, (i + 1) * P) for c in range(C)], x_parts, cols=part)
                if part.stop == T:
                    gates.then_inc(g_psum, 1)
                pe.wait_ge(piece_ready, order["u", e] + 1)
                wait(pe, hid_full_ready, m - 1)
                values = project(2 + m % 2, [cut(expert("u", e, C), c, i * P, (i + 1) * P) for c in range(C)], x_parts, cols=part)
                if part.stop == T:
                    values.then_inc(u_psum, 1)

            def down(m):
                e, i = m // IC, m % IC
                pe.wait_ge(piece_ready, order["d", e] + 1)
                pe.wait_ge(hid_ready, m + 1)
                if m == 0:
                    pe.wait_ge(xf_ready, TT)
                    pe.wait_ge(cw_ready, 1)
                for t in range(TT):
                    if e > 0 and i == 0:
                        pe.wait_ge(xs_added, terms_with(e - 1, t))
                    project(4 + t, [tuple(h[:, t * P:(t + 1) * P] for h in hid[m % 3])],
                                  [cut(expert("d", e, IC), i, 0, D)], starts=(i == 0),
                            stops=(i == IC - 1)).then_inc(down_psum, 1)

            first, second = slice(0, HALF), slice(HALF, T)
            transpose_x2(2)
            route_half(0)
            up(0, first)
            transpose_x2(3)
            up(1, first)
            route_half(1)
            up(0, second)
            pe.wait_ge(sig_ready, 1)
            pe.wait_ge(xf_ready, 2)
            for t in range(TT):
                ins = pe.transpose(bank[:, 5, t * E:(t + 1) * E], score_rows[:, t * P:(t + 1) * P], ident[0:E, 0:E])
            ins.then_inc(scoreT_psum, 1)
            up(1, second)
            for m in range(2, M):
                up(m)
                down(m - 2)
            pe.wait_ge(conv_ready, C)
            pe.wait_ge(silu_ready, M)
            pe.wait_ge(hid_full_ready, M)
            for t in range(TT):
                for c in range(C):
                    ins = pe.transpose(bank[:, t, c * P:(c + 1) * P], conv[:, c, t * P:(t + 1) * P], ident[:])
                ins.then_inc(conv_psum, 1)
            down(M - 2)
            down(M - 1)


def kernel(x, ctx_1024, L0_xattn_Wq, L0_xattn_bq, L0_xattn_Wk, L0_xattn_bk, L0_xattn_Wv, L0_xattn_bv, L0_xattn_Wo,
           L0_xattn_bo, L0_attn_W_qkv, L0_attn_qn_w, L0_attn_kn_w, L0_attn_W_out, L0_attn_b_out, L0_ffn_Wr,
           L0_ffn_router_bias, L0_ffn_Wg, L0_ffn_Wu, L0_ffn_Wd, L0_ffn_conv_w, L0_ffn_conv_b):
    import numpy as np
    import concourse.bacc as bacc
    from concourse.bass_utils import run_bass_kernel_spmd

    def on_partitions(w):
        w = np.asarray(w)
        return np.ascontiguousarray(w.reshape(-1, P, w.shape[-1]).transpose(1, 0, 2))

    def column(v):
        return np.asarray(v).reshape(-1, P).T

    ctx = np.asarray(ctx_1024)[0].reshape(NB, KC, P, C, P)
    wqkv = np.asarray(L0_attn_W_qkv)
    matrices = {"g": L0_ffn_Wg, "u": L0_ffn_Wu, "d": L0_ffn_Wd}
    arrays = {
        "x": np.ascontiguousarray(np.asarray(x)[0].reshape(TT, P, D)),
        "ctx_t": np.ascontiguousarray(ctx.transpose(0, 4, 3, 1, 2).reshape(NB, P, C, KB)),
        "ctx_n": np.ascontiguousarray(ctx.transpose(0, 2, 1, 3, 4).reshape(NB, P, KC, D)),
        "wq_t": np.ascontiguousarray(np.asarray(L0_xattn_Wq).reshape(C, P, C, P).transpose(0, 3, 2, 1).reshape(C, P, D)),
        "wk_in": on_partitions(L0_xattn_Wk),
        "wv_t": on_partitions(np.asarray(L0_xattn_Wv).T),
        "wo_t": on_partitions(np.asarray(L0_xattn_Wo).T),
        "wqkv_in": np.stack([on_partitions(wqkv[:, s * D:(s + 1) * D]) for s in range(3)]),
        "wout_in": on_partitions(L0_attn_W_out),
        "pieces": np.stack([on_partitions(np.asarray(matrices[kind])[e]).reshape(P, PIECE) for kind, e in PIECES]),
        "cols_in": np.ascontiguousarray(np.concatenate(
            [column(L0_xattn_bq), column(L0_xattn_bk), column(L0_xattn_bv), column(L0_attn_qn_w),
             column(L0_ffn_conv_b),
             np.asarray(L0_ffn_conv_w).reshape(TAPS, C, P).transpose(2, 1, 0).reshape(P, C * TAPS),
             on_partitions(L0_ffn_Wr).reshape(P, C * E)], axis=1)),
        "rows_in": np.concatenate([np.asarray(v).reshape(-1) for v in
                                   (L0_xattn_bo, L0_attn_kn_w, L0_attn_b_out, L0_ffn_router_bias)]),
    }
    nc = bacc.Bacc("TRN2", target_bir_lowering=False, num_devices=1)
    args = {name: nc.dram_tensor(name, a.shape, mybir.dt.from_np(a.dtype), kind="ExternalInput").ap()
            for name, a in arrays.items()}
    out = nc.dram_tensor("out", (TT, P, D), F32, kind="ExternalOutput").ap()
    perceiver_block(nc, **args, out=out)
    result = run_bass_kernel_spmd(nc, [arrays], core_ids=[0])
    return result.results[0]["out"].reshape(1, T, D)
```

```python
from contextlib import ExitStack

import concourse.bass as bass
from concourse import mybir

ALU = mybir.AluOpType
ACT = mybir.ActivationFunctionType
AX = mybir.AxisListType
F32 = mybir.dt.float32
F32R = mybir.dt.float32r

P = 128
D = 512
C = D // P
T = 512
TT = T // P
KEYS = 8192
KB = 512
NB = KEYS // KB
KC = KB // P
STEPS = NB * TT
GROUP = 2 * TT
GROUPS = STEPS // GROUP
HALF = T // 2
SCALE = float(D // 16) ** -0.5
LN_EPS = 1e-5
RMS_EPS = 1e-6
DEN_EPS = 1e-6
TOP_EPS = 1e-9
DH = 32
HG = P // DH
VW = P + HG
E = 8
EM = 4
HID = 256
IC = HID // P
M = EM * IC
TAPS = 4
WARM = 10
KEEP_WARM = 4
PAD = TAPS - 1
LOWEST = -3.0e38
ARENA = 184
PIECE = C * HID
PIECES = [("g", 0), ("u", 0), ("g", 1), ("u", 1), ("d", 0), ("g", 2), ("u", 2), ("d", 1), ("g", 3), ("u", 3),
          ("d", 2), ("d", 3)]

COLS = {}
NCOLS = 0
for _name, _n in (("bq", C), ("bk", C), ("bv", C), ("qn", C), ("conv_b", C), ("conv_w", C * TAPS), ("wr", C * E)):
    COLS[_name] = NCOLS
    NCOLS += _n
ROWS = {"bo": (0, D), "kn": (D, 2 * D), "b_out": (2 * D, 3 * D), "rb": (3 * D, 3 * D + E)}
NROWS = 3 * D + E


def perceiver_block(nc, x, ctx_t, ctx_n, wq_t, wk_in, wv_t, wo_t, wqkv_in, wout_in, pieces, cols_in, rows_in, out):
    with ExitStack() as stack:
        def sb(name, shape, dt=F32, on=stack):
            return on.enter_context(nc.sbuf_tensor(name, shape, dt))

        def sem(name):
            return stack.enter_context(nc.semaphore(name))

        bank = stack.enter_context(nc.psum_tensor("bank", [P, 8, 512], F32))

        ident = sb("ident", [P, P])
        cols = sb("cols", [P, NCOLS])
        rows = sb("rows", [P, NROWS])
        xs = sb("xs", [P, TT, D])
        xn = sb("xn", [P, TT, D])
        stats = sb("stats", [P, TT, 6])
        mv = sb("mv", [P, TT, 2])
        var = sb("var", [P, TT])
        std = sb("std", [P, TT])
        rstd = sb("rstd", [P, TT])
        ones = sb("ones", [P, 1])
        shift = sb("shift", [P, TT])
        arena = sb("arena", [P, ARENA * 256])
        base = nc.sbuf_base - ARENA * 1024

        def col(name, i):
            a = COLS[name] + i
            return cols[:, a:a + 1]

        def row(name):
            a, b = ROWS[name]
            return rows[:, a:b]

        def at(kib, name, shape, dt=F32):
            size = 4
            for n in shape[1:]:
                size *= n
            assert kib * 1024 + size <= ARENA * 1024
            return nc.alloc_sbuf_tensor_at(name, shape, dt, offset=base + int(kib * 1024))

        def parts(kib, name, shape):
            size = 4
            for n in shape[1:]:
                size *= n
            return at(kib, name + "_h", shape, F32R), at(kib + size / 1024, name + "_l", shape, F32R)

        xT = parts(0, "xT", [P, C, T])
        wq = parts(16, "wq", [P, C, D])
        wk = parts(32, "wk", [P, C, D])
        wq_raw = at(144, "wq_raw", [P, C, D])
        wk_raw = at(152, "wk_raw", [P, C, D])
        qT = parts(112, "qT", [P, C, T])
        qb = at(164, "qb", [P, C, T])
        wv_raw = at(0, "wv_raw", [P, C, D])
        wo_raw = at(8, "wo_raw", [P, C, D])
        wv = parts(16, "wv", [P, C, D])
        wo = parts(32, "wo", [P, C, D])
        qk = parts(48, "qk", [P, C, T])
        raw_t = [at(64 + 8 * b, f"raw_t{b}", [P, C, KB]) for b in range(2)]
        raw_n = [at(80 + 8 * b, f"raw_n{b}", [P, KC, D]) for b in range(2)]
        ct = [parts(96 + 16 * b, f"ct{b}", [P, C, KB]) for b in range(2)]
        cn = [parts(128 + 16 * b, f"cn{b}", [P, KC, D]) for b in range(2)]
        probs = [at(160 + 2 * b, f"probs{b}", [P, KB]) for b in range(2)]
        pt = [parts(164 + 4 * b, f"pt{b}", [P, KC, P]) for b in range(2)]
        acc = xn
        small = at(175.5, "small", [P, 11 * TT])

        def stat(n, width=1):
            return small[:, n * TT:(n + width) * TT]

        run_max = stat(0, 2).rearrange("p (m t) -> p m t", m=2)
        block_max, neg_max, exp_bias, key_bias, alpha, row_sum, den, inv_den = (stat(n) for n in range(2, 10))
        kvmask = at(172.5, "kvmask", [P, VW])
        lower = at(173.25, "lower", [P, E, E])
        wr = parts(175.6875, "wr", [P, C, E])
        wqkv = [ct[0], cn[0], ct[1]]
        wout = cn[1]
        vT = parts(48, "vT", [P, C, T])
        square = at(48, "square", [P, D])
        qs = at(64, "qs", [P, TT, D])
        ks = at(72, "ks", [P, TT, D])
        vs = at(80, "vs", [P, TT, C, VW])
        qrT = at(160, "qrT", [P, C, T])
        kv = at(168.25, "kv", [P, C, VW])
        heads = qs
        late = at(62, "late", [P, 512])

        def late_stat(a, *dims):
            n = 1
            for d in dims:
                n *= d
            v = late[:, a:a + n]
            names = " ".join("abc"[:len(dims)])
            sizes = {"abc"[i]: dims[i] for i in range(len(dims))}
            return v.rearrange(f"p ({names}) -> p {names}", **sizes) if len(dims) > 1 else v

        ssq = late_stat(0, TT, 2)
        rms = late_stat(8, TT, 2)
        rrms = late_stat(16, TT, 2)
        norm = late_stat(32, TT, C, HG)
        rnorm = late_stat(96, TT, C, HG)
        sig = late_stat(160, TT, E)
        biased = late_stat(192, TT, E)
        rank = late_stat(224, TT, E)
        gate = late_stat(256, TT, E)
        cw = late_stat(288, TT, E)
        gsum = late_stat(320, TT)
        grec = late_stat(324, TT)
        cw_id = late_stat(328, TT)
        piece_raw = [at(176 + 4 * b, f"piece_raw{b}", [P, PIECE]) for b in range(2)]
        piece = [parts(k, f"piece{n}", [P, PIECE]) for n, k in enumerate((16, 24, 32, 40, 96, 104, 112, 120, 128, 136, 144, 152))]
        order = {(kind, e): n for n, (kind, e) in enumerate(PIECES)}
        xf = at(160, "xf", [P, C, PAD + T])
        score_rows = at(168.25, "score_rows", [E, T])
        above = at(170.25, "above", [P, TT, E, E])
        tied = at(171.25, "tied", [P, TT, E, E])
        conv = at(48, "conv", [P, C, T])
        relu_x = at(56, "relu_x", [P, 2, D])
        hid = [parts(64 + 4 * b, f"hid{b}", [P, T]) for b in range(3)]
        hid_full = [at(76 + 2 * b, f"hid_full{b}", [P, T]) for b in range(2)]
        act_g = [at(80 + 2 * b, f"act_g{b}", [P, T]) for b in range(2)]

        x_loaded = [sem(f"x_loaded{t}") for t in range(TT)]
        cols_loaded = sem("cols_loaded")
        rows_loaded = sem("rows_loaded")
        wq_loaded = [sem(f"wq_loaded{e}") for e in range(C)]
        wk_loaded = sem("wk_loaded")
        wv_loaded = sem("wv_loaded")
        wo_loaded = sem("wo_loaded")
        piece_loaded = [sem(f"piece_loaded{b}") for b in range(2)]
        piece_high = sem("piece_high")
        piece_ready = sem("piece_ready")
        wq_high = sem("wq_high")
        wq_ready = sem("wq_ready")
        wk_high = sem("wk_high")
        wk_ready = sem("wk_ready")
        wvo_high = sem("wvo_high")
        wvo_ready = sem("wvo_ready")
        raw_loaded = [sem(f"raw_loaded{b}") for b in range(2)]
        out_stored = sem("out_stored")

        ident_ready = sem("ident_ready")
        ones_ready = sem("ones_ready")
        pads_ready = sem("pads_ready")
        masks_ready = sem("masks_ready")
        bo_added = sem("bo_added")
        ln_step = sem("ln_step")
        var_ready = sem("var_ready")
        std_ready = sem("std_ready")
        shift_ready = sem("shift_ready")
        xn_ready = sem("xn_ready")
        xnT_psum = sem("xnT_psum")
        xh_ready = sem("xh_ready")
        xl_ready = sem("xl_ready")
        xf_ready = sem("xf_ready")
        q_psum = sem("q_psum")
        qTh_ready = sem("qTh_ready")
        qTl_ready = sem("qTl_ready")
        qb_step = sem("qb_step")
        acc_cleared = sem("acc_cleared")
        wr_high = sem("wr_high")
        wr_ready = sem("wr_ready")
        qk_psum = sem("qk_psum")
        qkh_ready = sem("qkh_ready")
        qkl_ready = sem("qkl_ready")
        keyb_psum = sem("keyb_psum")
        init_done = sem("init_done")

        ctxh_ready = sem("ctxh_ready")
        ctxl_ready = sem("ctxl_ready")
        s_done = sem("s_done")
        max_step = sem("max_step")
        bias_ready = sem("bias_ready")
        exp_done = sem("exp_done")
        alpha_ready = sem("alpha_ready")
        t_done = sem("t_done")
        pth_ready = sem("pth_ready")
        ptl_ready = sem("ptl_ready")
        pv_done = sem("pv_done")
        acc_done = sem("acc_done")
        den_done = sem("den_done")
        inv_ready = sem("inv_ready")

        v_psum = sem("v_psum")
        vTh_ready = sem("vTh_ready")
        vTl_ready = sem("vTl_ready")
        y_psum = sem("y_psum")
        x1_ready = sem("x1_ready")
        bout_added = sem("bout_added")
        q2_psum = sem("q2_psum")
        k2_psum = sem("k2_psum")
        v2_psum = sem("v2_psum")
        q_ssq = sem("q_ssq")
        ms_ready = sem("ms_ready")
        rms_ready = sem("rms_ready")
        rrms_ready = sem("rrms_ready")
        qs_ready = sem("qs_ready")
        kw_ready = sem("kw_ready")
        k_ready = sem("k_ready")
        v_ready = sem("v_ready")
        qsT_psum = sem("qsT_psum")
        qrT_ready = sem("qrT_ready")
        kv_psum = sem("kv_psum")
        kv_ready = sem("kv_ready")
        la_psum = sem("la_psum")
        norm_ready = sem("norm_ready")
        rnorm_ready = sem("rnorm_ready")
        heads_ready = sem("heads_ready")
        z_psum = sem("z_psum")
        x2_ready = sem("x2_ready")
        route_psum = sem("route_psum")
        sig_ready = sem("sig_ready")
        route_step = sem("route_step")
        scoreT_psum = sem("scoreT_psum")
        cw_ready = sem("cw_ready")
        xs_added = sem("xs_added")
        relu_ready = sem("relu_ready")
        conv_step = sem("conv_step")
        conv_ready = sem("conv_ready")
        g_psum = sem("g_psum")
        u_psum = sem("u_psum")
        silu_ready = sem("silu_ready")
        hid_full_ready = sem("hid_full_ready")
        hidh_ready = sem("hidh_ready")
        hid_ready = sem("hid_ready")
        down_psum = sem("down_psum")
        conv_psum = sem("conv_psum")
        out_ready = sem("out_ready")

        def wait(eng, s, n):
            if isinstance(n, int) and n <= 0:
                return
            eng.wait_ge(s, n)

        def over_steps(eng, step):
            for i in range(GROUP):
                step(i, i)
            with eng.Fori(1, GROUPS - 1) as g:
                for u in range(GROUP):
                    step(g * GROUP + u, u)
            for u in range(GROUP):
                step(STEPS - GROUP + u, u, last=True)

        block = stack.enter_context(nc.Block())

        @block.sync
        def _(sp):
            for t in range(0, TT, 2):
                for n in range(t, t + 2):
                    sp.dma_start(xs[:, n, :], x[n]).then_inc(x_loaded[n], 16)
                for e in range(t, t + 2):
                    sp.dma_start(wq_raw[:, e, :], wq_t[e]).then_inc(wq_loaded[e], 16)
            sp.dma_start(cols[:], cols_in).then_inc(cols_loaded, 16)
            sp.dma_start(wk_raw[:], wk_in).then_inc(wk_loaded, 16)
            for b in range(2):
                sp.dma_start(raw_t[b][:], ctx_t[b]).then_inc(raw_loaded[b], 16)
                sp.dma_start(raw_n[b][:], ctx_n[b]).then_inc(raw_loaded[b], 16)
            sp.dma_start(rows[:], rows_in.partition_broadcast(P)).then_inc(rows_loaded, 16)
            sp.wait_ge(q_psum, 2 * C)
            sp.dma_start(wv_raw[:], wv_t).then_inc(wv_loaded, 16)
            sp.dma_start(wo_raw[:], wo_t).then_inc(wo_loaded, 16)
            for n in range(2):
                sp.dma_start(piece_raw[n][:], pieces[n]).then_inc(piece_loaded[n], 16)
            with sp.Fori(1, NB // 2) as g:
                for b in range(2):
                    sp.wait_ge(ctxl_ready, g * (2 * TT) + (b - 1) * TT)
                    sp.dma_start(raw_t[b][:], ctx_t[bass.ds(g * 2 + b, 1)].rearrange("a p c k -> (a p) c k")).then_inc(raw_loaded[b], 16)
                    sp.dma_start(raw_n[b][:], ctx_n[bass.ds(g * 2 + b, 1)].rearrange("a p c k -> (a p) c k")).then_inc(raw_loaded[b], 16)
            for b in range(2):
                sp.wait_ge(ctxl_ready, (NB - 1 + b) * TT)
                sp.dma_start(raw_t[b][:], wqkv_in[2 * b]).then_inc(raw_loaded[b], 16)
                sp.dma_start(raw_n[b][:], wqkv_in[1] if b == 0 else wout_in).then_inc(raw_loaded[b], 16)
            for n in range(2, len(PIECES)):
                sp.wait_ge(piece_ready, n - 1)
                sp.dma_start(piece_raw[n % 2][:], pieces[n]).then_inc(piece_loaded[n % 2], 16)
            for t in range(TT):
                sp.wait_ge(out_ready, t + 1)
                sp.dma_start(out[t], xs[:, t, :]).then_inc(out_stored, 16)
            sp.wait_ge(out_stored, 16 * TT)

        @block.gpsimd
        def _(pool):
            pool.memset(ident[:], 0.0).then_inc(ident_ready, 1)
            pool.wait_ge(ident_ready, 1)
            pool.affine_select(out=ident[:], in_=ident[:], compare_op=ALU.not_equal, fill=1.0, base=0,
                               pattern=[[-1, P]], channel_multiplier=1).then_inc(ident_ready, 1)
            for e in range(C):
                pool.wait_ge(wq_high, e + 1)
                pool.tensor_tensor(wq[1][:, e, :], wq_raw[:, e, :], wq[0][:, e, :].bitcast(F32), ALU.subtract).then_inc(wq_ready, 1)
            pool.wait_ge(wk_high, 1)
            pool.tensor_tensor(wk[1][:], wk_raw[:], wk[0][:].bitcast(F32), ALU.subtract).then_inc(wk_ready, 1)
            pool.memset(ones[:], 1.0).then_inc(ones_ready, 1)
            pool.wait_ge(cols_loaded, 16)
            a = COLS["wr"]
            pool.tensor_copy(wr[0][:].rearrange("p c e -> p (c e)"), cols[:, a:a + C * E]).then_inc(wr_high, 1)
            pool.wait_ge(wr_high, 1)
            pool.tensor_tensor(wr[1][:].rearrange("p c e -> p (c e)"), cols[:, a:a + C * E],
                               wr[0][:].rearrange("p c e -> p (c e)").bitcast(F32), ALU.subtract).then_inc(wr_ready, 1)
            pool.wait_ge(xnT_psum, TT)
            pool.memset(acc[:], 0.0).then_inc(acc_cleared, 1)
            pool.wait_ge(rows_loaded, 16)
            pool.wait_ge(xn_ready, TT)
            for t in range(TT):
                pool.tensor_tensor(xs[:, t, :], xs[:, t, :], row("bo"), ALU.add).then_inc(bo_added, 1)
            pool.wait_ge(qk_psum, 2 * C)
            for n, (raw, w, loaded) in enumerate(((wv_raw, wv, wv_loaded), (wo_raw, wo, wo_loaded))):
                pool.wait_ge(loaded, 16)
                pool.tensor_copy(w[0][:], raw[:]).then_inc(wvo_high, 1)
                pool.wait_ge(wvo_high, n + 1)
                pool.tensor_tensor(w[1][:], raw[:], w[0][:].bitcast(F32), ALU.subtract).then_inc(wvo_ready, 1)
            pool.memset(kvmask[:], 0.0).then_inc(masks_ready, 1)
            pool.memset(lower[:], 0.0).then_inc(masks_ready, 1)
            pool.wait_ge(masks_ready, 2)
            made = 2
            for h in range(HG):
                pool.memset(kvmask[h * DH:(h + 1) * DH, h * DH:(h + 1) * DH], 1.0).then_inc(masks_ready, 1)
                made += 1
                pool.wait_ge(masks_ready, made)
                pool.memset(kvmask[h * DH:(h + 1) * DH, P + h:P + h + 1], 1.0).then_inc(masks_ready, 1)
                made += 1
                pool.wait_ge(masks_ready, made)
            for e in range(1, E):
                pool.memset(lower[:, e, 0:e], 1.0).then_inc(masks_ready, 1)
                made += 1
                pool.wait_ge(masks_ready, made)
            pool.wait_ge(ctxl_ready, (NB + 2) * TT)
            pool.memset(vs[:, :, :, P:VW], 1.0).then_inc(pads_ready, 1)

            def split_piece(n):
                pool.wait_ge(piece_loaded[n % 2], 16 * (n // 2 + 1))
                pool.tensor_copy(piece[n][0][:], piece_raw[n % 2][:]).then_inc(piece_high, 1)
                pool.wait_ge(piece_high, n + 1)
                pool.tensor_tensor(piece[n][1][:], piece_raw[n % 2][:], piece[n][0][:].bitcast(F32),
                                   ALU.subtract).then_inc(piece_ready, 1)

            pool.wait_ge(y_psum, TT)
            for n in range(0, 4):
                split_piece(n)
            pool.wait_ge(xn_ready, 3 * TT)
            for t in range(TT):
                pool.tensor_tensor(xs[:, t, :], xs[:, t, :], row("b_out"), ALU.add).then_inc(bout_added, 1)
            pool.wait_ge(v2_psum, TT)
            for n in range(4, 8):
                split_piece(n)
            pool.wait_ge(la_psum, TT)
            pool.memset(xf[:, :, 0:PAD], 0.0).then_inc(pads_ready, 1)
            for n in range(8, 10):
                split_piece(n)
            pool.wait_ge(z_psum, TT)
            for n in range(10, 12):
                split_piece(n)

        def terms_with(e, t):
            return e * TT + t + 1 + 2 * min(TT, IC * (e + 1))

        XT_BANKS = (0, 1, 2, 3)
        Q_BANKS = ((4, 5, 6, 7), (0, 1, 2, 3))
        ON_BANKS = (6, 7, 0, 1)
        V_BANKS = ((2, 3, 4, 5), (6, 7, 0, 1))
        Y_BANKS = (2, 3, 4, 5)
        X1_BANKS = (6, 7, 0, 1)
        KQV_BANKS = (2, 3, 4, 5, 6, 7)
        QT_BANKS = (0, 1)
        KV_BANKS = (2, 3, 4, 5)
        LA_BANKS = (6, 0, 2, 4)
        HEAD_BANKS = (6, 7, 0, 1)
        X2_BANKS = (4, 5, 6, 7)
        MASKS = 2 + 2 * HG + E - 1

        @block.scalar
        def _(act):
            def std_of(n):
                t = n % TT
                act.wait_ge(var_ready, n + 1)
                act.activation(std[:, t:t + 1], var[:, t:t + 1], ACT.Sqrt).then_inc(std_ready, 1)

            def high_xT(n, banks):
                t = n % TT
                act.wait_ge(xnT_psum, n + 1)
                act.copy(xT[0][:, :, t * P:(t + 1) * P],
                         bank[:, banks[t], :].rearrange("p (c t) -> p c t", c=C)).then_inc(xh_ready, 1)

            def apply_of(n):
                t = n % TT
                act.wait_ge(shift_ready, n + 1)
                act.activation(xn[:, t, :], xs[:, t, :], ACT.Identity, bias=shift[:, t:t + 1],
                               scale=rstd[:, t:t + 1]).then_inc(xn_ready, 1)

            def high_wq(e):
                act.wait_ge(wq_loaded[e], 16)
                act.copy(wq[0][:, e, :], wq_raw[:, e, :]).then_inc(wq_high, 1)

            std_of(0)
            apply_of(0)
            high_wq(0)
            std_of(1)
            apply_of(1)
            high_xT(0, XT_BANKS)
            std_of(2)
            high_xT(1, XT_BANKS)
            high_wq(1)
            apply_of(2)
            std_of(3)
            high_wq(2)
            high_xT(2, XT_BANKS)
            apply_of(3)
            high_wq(3)
            high_xT(3, XT_BANKS)
            act.wait_ge(wk_loaded, 16)
            act.copy(wk[0][:], wk_raw[:]).then_inc(wk_high, 1)
            def high_block(u):
                src, dst = (raw_t[0], ct[0][0]) if u < 2 else (raw_n[0], cn[0][0])
                v = 2 * (u % 2)
                act.copy(dst[:, v:v + 2, :], src[:, v:v + 2, :]).then_inc(ctxh_ready, 1)

            def high_q(n):
                c, h = n % C, n // C * HALF
                act.wait_ge(q_psum, n + 1)
                act.activation(qT[0][:, c, h:h + HALF], bank[:, Q_BANKS[n // C][c], h:h + HALF], ACT.Identity,
                               bias=col("bq", c)).then_inc(qTh_ready, 1)

            act.wait_ge(cols_loaded, 16)
            for n in range(C):
                high_q(n)
            act.wait_ge(raw_loaded[0], 32)
            for n in range(C):
                high_block(n)
                high_q(C + n)
            for n in range(2 * C):
                c, h = n % C, n // C * HALF
                act.wait_ge(qk_psum, n + 1)
                act.copy(qk[0][:, c, h:h + HALF], bank[:, Q_BANKS[n // C][c], h:h + HALF]).then_inc(qkh_ready, 1)

            def step(i, u, last=False):
                if not (isinstance(i, int) and i == 0):
                    b = (u - 1) % 2
                    wait(act, t_done, i)
                    wait(act, pv_done, i - 2)
                    act.copy(pt[b][0][:], bank[:, 2 + b, :].rearrange("p (c k) -> p c k", c=KC)).then_inc(pth_ready, 1)
                if isinstance(i, int) and i >= STEPS:
                    return
                t, b, m = u % TT, u % 2, (u // TT) % 2
                act.wait_ge(bias_ready, i + 1)
                act.activation(probs[b][:], bank[:, b, :], ACT.Exp, bias=exp_bias[:, t:t + 1], scale=SCALE,
                               accum_out=row_sum[:, t:t + 1]).then_inc(exp_done, 1)
                act.activation(alpha[:, t:t + 1], run_max[:, m, t:t + 1], ACT.Exp, bias=neg_max[:, t:t + 1],
                               scale=SCALE).then_inc(alpha_ready, 1)
                next_high(i, t, 1 - m)

            def next_high(i, t, nb):
                if t == 0:
                    act.wait_ge(raw_loaded[nb], (i + TT - nb * TT) * 4 + 32)
                if t < 2:
                    wait(act, s_done, i - t)
                    act.copy(ct[nb][0][:, 2 * t:2 * t + 2, :], raw_t[nb][:, 2 * t:2 * t + 2, :]).then_inc(ctxh_ready, 1)
                else:
                    v = 2 * (t - 2)
                    wait(act, pv_done, i - t)
                    act.copy(cn[nb][0][:, v:v + 2, :], raw_n[nb][:, v:v + 2, :]).then_inc(ctxh_ready, 1)

            over_steps(act, step)
            step(STEPS, 0, last=True)

            act.wait_ge(wvo_ready, 2)
            high_xT(TT + 0, ON_BANKS)
            high_xT(TT + 1, ON_BANKS)
            next_high(STEPS, 0, 1)
            high_xT(TT + 2, ON_BANKS)
            high_xT(TT + 3, ON_BANKS)
            next_high(STEPS + 1, 1, 1)
            for n in range(2 * C):
                c, h = n % C, n // C * HALF
                act.wait_ge(v_psum, n + 1)
                act.activation(vT[0][:, c, h:h + HALF], bank[:, V_BANKS[n // C][c], h:h + HALF], ACT.Identity,
                               bias=col("bv", c)).then_inc(vTh_ready, 1)
                if C <= n < C + 2:
                    next_high(STEPS + n - C + 2, n - C + 2, 1)
            for t in range(TT):
                if t >= 2:
                    high_xT(2 * TT + t - 2, X1_BANKS)
                std_of(TT + t)
                apply_of(TT + t)
            act.wait_ge(ctxl_ready, (NB + 2) * TT)

            def root(t, s):
                act.wait_ge(ms_ready, 2 * t + s + 1)
                act.activation(rms[:, t, s:s + 1], rms[:, t, s:s + 1], ACT.Sqrt).then_inc(rms_ready, 1)

            def square_of(t, s, done):
                act.wait_ge(done, t + 1)
                wait(act, q_ssq, 2 * t + s)
                act.activation(square[:], bank[:, KQV_BANKS[(3 * t + s) % 6], :], ACT.Square,
                               accum_out=ssq[:, t, s:s + 1]).then_inc(q_ssq, 1)
                root(t, s)

            def queries(t):
                act.wait_ge(qsT_psum, t + 1)
                for c in range(C):
                    ins = act.activation(qrT[:, c, t * P:(t + 1) * P], bank[:, QT_BANKS[t % 2], c * P:(c + 1) * P],
                                         ACT.Relu, scale=col("qn", c))
                ins.then_inc(qrT_ready, 1)

            for t in range(TT):
                square_of(t, 0, k2_psum)
                square_of(t, 1, q2_psum)
                act.wait_ge(rrms_ready, 2 * t + 2)
                act.activation(qs[:, t, :], bank[:, KQV_BANKS[(3 * t + 1) % 6], :], ACT.Copy,
                               scale=rrms[:, t, 1:2]).then_inc(qs_ready, 1)
                act.wait_ge(v2_psum, t + 1)
                act.copy(vs[:, t, :, 0:P],
                         bank[:, KQV_BANKS[(3 * t + 2) % 6], :].rearrange("p (c k) -> p c k", c=C)).then_inc(v_ready, 1)
                if t < 2:
                    high_xT(2 * TT + t + 2, X1_BANKS)
                if t >= 1:
                    queries(t - 1)
            queries(TT - 1)
            for t in range(TT - 1):
                high_xT(3 * TT + t, HEAD_BANKS)

            def whole_xT(t):
                act.wait_ge(xl_ready, 4 * TT + t + 1)
                act.copy(xf[:, :, PAD + t * P:PAD + (t + 1) * P],
                         bank[:, X2_BANKS[t], :].rearrange("p (c t) -> p c t", c=C)).then_inc(xf_ready, 1)

            std_of(2 * TT)
            apply_of(2 * TT)
            high_xT(3 * TT + 3, HEAD_BANKS)
            std_of(2 * TT + 1)
            apply_of(2 * TT + 1)
            high_xT(4 * TT, X2_BANKS)
            std_of(2 * TT + 2)
            high_xT(4 * TT + 1, X2_BANKS)
            apply_of(2 * TT + 2)
            high_xT(4 * TT + 2, X2_BANKS)
            std_of(2 * TT + 3)
            apply_of(2 * TT + 3)
            high_xT(4 * TT + 3, X2_BANKS)
            for t in range(TT):
                whole_xT(t)

            def high_hid(m):
                act.wait_ge(hid_full_ready, m + 1)
                wait(act, down_psum, (m - 2) * TT)
                act.copy(hid[m % 3][0][:], hid_full[m % 2][:]).then_inc(hidh_ready, 1)

            for m in range(M):
                act.wait_ge(g_psum, m + 1)
                wait(act, hid_full_ready, m - 1)
                act.activation(act_g[m % 2][:], bank[:, m % 2, :], ACT.Silu).then_inc(silu_ready, 1)
                if m >= 1:
                    high_hid(m - 1)
                if m == 1:
                    act.wait_ge(route_psum, 1)
                    act.activation(score_rows[:], bank[0:E, 4, :], ACT.Sigmoid).then_inc(sig_ready, 1)
                if 2 <= m < 2 + TT:
                    t = m - 2
                    act.wait_ge(cw_ready, 1)
                    wait(act, xs_added, 2 * (t - 1))
                    act.activation(relu_x[:, t % 2, :], xn[:, t, :], ACT.Relu, scale=cw[:, t, 7:8]).then_inc(relu_ready, 1)
            high_hid(M - 1)

        @block.vector
        def _(dve):
            lnc = [0]

            def ln_chain(ins):
                ins.then_inc(ln_step, 1)
                lnc[0] += 1
                dve.wait_ge(ln_step, lnc[0])

            def ln_stats(n):
                t = n % TT
                ln_chain(dve.bn_stats(stats[:, t, :], xs[:, t, :]))
                ln_chain(dve.bn_aggr(mv[:, t, :], stats[:, t, :]))
                dve.tensor_scalar(var[:, t:t + 1], mv[:, t, 1:2], LN_EPS, None, ALU.add).then_inc(var_ready, 1)

            def ln_scale(n):
                t = n % TT
                dve.wait_ge(std_ready, n + 1)
                ln_chain(dve.reciprocal(rstd[:, t:t + 1], std[:, t:t + 1]))
                dve.tensor_scalar(shift[:, t:t + 1], mv[:, t, 0:1], rstd[:, t:t + 1], -1.0, ALU.mult,
                                  ALU.mult).then_inc(shift_ready, 1)

            def low_xT(n, banks):
                t = n % TT
                dve.wait_ge(xh_ready, n + 1)
                dve.tensor_tensor(xT[1][:, :, t * P:(t + 1) * P],
                                  bank[:, banks[t], :].rearrange("p (c t) -> p c t", c=C),
                                  xT[0][:, :, t * P:(t + 1) * P].bitcast(F32), ALU.subtract).then_inc(xl_ready, 1)

            def first_stats(t):
                dve.wait_ge(x_loaded[t], 16)
                ln_stats(t)

            first_stats(0)
            ln_scale(0)
            first_stats(1)
            ln_scale(1)
            first_stats(2)
            low_xT(0, XT_BANKS)
            ln_scale(2)
            low_xT(1, XT_BANKS)
            first_stats(3)
            ln_scale(3)
            low_xT(2, XT_BANKS)
            low_xT(3, XT_BANKS)

            def split_low(t, b, q):
                dve.wait_ge(ctxh_ready, q + 1)
                raw, split = (raw_t, ct) if t < 2 else (raw_n, cn)
                v = 2 * (t % 2)
                dve.tensor_tensor(split[b][1][:, v:v + 2, :], raw[b][:, v:v + 2, :],
                                  split[b][0][:, v:v + 2, :].bitcast(F32),
                                  ALU.subtract).then_inc(ctxl_ready, 1)

            dve.wait_ge(cols_loaded, 16)

            def low_q(n):
                c, h = n % C, n // C * HALF
                dve.wait_ge(qTh_ready, n + 1)
                dve.tensor_scalar(qb[:, c, h:h + HALF], bank[:, Q_BANKS[n // C][c], h:h + HALF], col("bq", c),
                                  col("bk", c), ALU.add, ALU.mult).then_inc(qb_step, 1)
                dve.scalar_tensor_tensor(out=qT[1][:, c, h:h + HALF], in0=bank[:, Q_BANKS[n // C][c], h:h + HALF],
                                         scalar=col("bq", c), in1=qT[0][:, c, h:h + HALF].bitcast(F32), op0=ALU.add,
                                         op1=ALU.subtract).then_inc(qTl_ready, 1)

            def low_qk(n):
                c, h = n % C, n // C * HALF
                dve.wait_ge(qkh_ready, n + 1)
                dve.tensor_tensor(qk[1][:, c, h:h + HALF], bank[:, Q_BANKS[n // C][c], h:h + HALF],
                                  qk[0][:, c, h:h + HALF].bitcast(F32), ALU.subtract).then_inc(qkl_ready, 1)

            for n in range(C):
                low_q(n)
            for n in range(C):
                if n < TT - 1:
                    split_low(n, 0, n)
                low_q(C + n)
            dve.memset(run_max[:, 0, :], LOWEST).then_inc(init_done, 1)
            dve.memset(den[:], 0.0).then_inc(init_done, 1)
            low_qk(0)
            dve.wait_ge(qb_step, 2 * C)
            dve.tensor_tensor(qb[:, 0:2, :], qb[:, 0:2, :], qb[:, 2:4, :], ALU.add).then_inc(qb_step, 1)
            low_qk(1)
            dve.wait_ge(qb_step, 2 * C + 1)
            dve.tensor_tensor(qb[:, 0, :], qb[:, 0, :], qb[:, 1, :], ALU.add).then_inc(qb_step, 1)
            for n in range(2, 2 * C):
                low_qk(n)
            dve.wait_ge(keyb_psum, 1)
            dve.tensor_copy(key_bias[:], bank[:, 4, 0:TT]).then_inc(init_done, 1)
            dve.wait_ge(init_done, 3)
            dve.wait_ge(acc_cleared, 1)

            def step(i, u, last=False):
                if not (isinstance(i, int) and i < 3):
                    t, b = (u - 3) % TT, (u - 3) % 2
                    dve.wait_ge(pv_done, i - 2)
                    dve.wait_ge(alpha_ready, i - 2)
                    wait(dve, den_done, i - 3)
                    dve.scalar_tensor_tensor(out=acc[:, t, :], in0=acc[:, t, :], scalar=alpha[:, t:t + 1],
                                             in1=bank[:, 4 + b, :], op0=ALU.mult, op1=ALU.add).then_inc(acc_done, 1)
                    dve.scalar_tensor_tensor(out=den[:, t:t + 1], in0=den[:, t:t + 1], scalar=alpha[:, t:t + 1],
                                             in1=row_sum[:, t:t + 1], op0=ALU.mult, op1=ALU.add).then_inc(den_done, 1)
                    if last and i - 3 >= STEPS - TT:
                        dve.wait_ge(den_done, i - 2)
                        dve.reciprocal(inv_den[:, t:t + 1], den[:, t:t + 1]).then_inc(inv_ready, 1)
                        dve.wait_ge(inv_ready, t + 1)
                        dve.tensor_scalar(acc[:, t, :], acc[:, t, :], inv_den[:, t:t + 1], None, ALU.mult).then_inc(xn_ready, 1)
                live = not (isinstance(i, int) and i >= STEPS)
                t, b, m = u % TT, u % 2, (u // TT) % 2
                early = isinstance(i, int) and i < 2
                if live and not early:
                    split_low((t - 1) % TT, m if t == 0 else 1 - m, i + 3)
                if live:
                    dve.wait_ge(s_done, i + 1)
                    dve.reduce_max(block_max[:, t:t + 1], bank[:, b, :], AX.X).then_inc(max_step, 1)
                    dve.wait_ge(max_step, i * 2 + 1)
                    dve.tensor_scalar(run_max[:, 1 - m, t:t + 1], block_max[:, t:t + 1], key_bias[:, t:t + 1],
                                      run_max[:, m, t:t + 1], ALU.add, ALU.max).then_inc(max_step, 1)
                    dve.wait_ge(max_step, i * 2 + 2)
                    dve.tensor_scalar(neg_max[:, t:t + 1], run_max[:, 1 - m, t:t + 1], -SCALE, None, ALU.mult)
                    dve.tensor_scalar(exp_bias[:, t:t + 1], run_max[:, 1 - m, t:t + 1], key_bias[:, t:t + 1], -SCALE,
                                      ALU.subtract, ALU.mult).then_inc(bias_ready, 1)
                if early:
                    split_low((t - 1) % TT, m if t == 0 else 1 - m, i + 3)
                if not (isinstance(i, int) and (i == 0 or i > STEPS)):
                    b = (u - 1) % 2
                    dve.wait_ge(pth_ready, i)
                    dve.tensor_tensor(pt[b][1][:], bank[:, 2 + b, :].rearrange("p (c k) -> p c k", c=KC),
                                      pt[b][0][:].bitcast(F32), ALU.subtract).then_inc(ptl_ready, 1)

            over_steps(dve, step)
            step(STEPS, 0, last=True)
            low_xT(TT + 0, ON_BANKS)
            split_low(TT - 1, 0, STEPS + TT - 1)
            step(STEPS + 1, 1, last=True)
            low_xT(TT + 1, ON_BANKS)
            step(STEPS + 2, 2, last=True)
            low_xT(TT + 2, ON_BANKS)
            split_low(0, 1, STEPS + TT)
            low_xT(TT + 3, ON_BANKS)
            for n in range(2 * C):
                c, h = n % C, n // C * HALF
                dve.wait_ge(vTh_ready, n + 1)
                dve.scalar_tensor_tensor(out=vT[1][:, c, h:h + HALF], in0=bank[:, V_BANKS[n // C][c], h:h + HALF],
                                         scalar=col("bv", c), in1=vT[0][:, c, h:h + HALF].bitcast(F32), op0=ALU.add,
                                         op1=ALU.subtract).then_inc(vTl_ready, 1)
                if C - 1 <= n < C + 2:
                    split_low(n - C + 2, 1, STEPS + TT + n - C + 2)
            dve.wait_ge(bo_added, TT)
            for t in range(TT):
                dve.wait_ge(y_psum, t + 1)
                dve.tensor_tensor(xs[:, t, :], xs[:, t, :], bank[:, Y_BANKS[t], :], ALU.add).then_inc(x1_ready, 1)
                dve.wait_ge(x1_ready, t + 1)
                ln_stats(TT + t)
                ln_scale(TT + t)
                if t >= 2:
                    low_xT(2 * TT + t - 2, X1_BANKS)

            def over_rms(t, s):
                n = 2 * t + s
                dve.wait_ge(q_ssq, n + 1)
                dve.tensor_scalar(rms[:, t, s:s + 1], ssq[:, t, s:s + 1], 1.0 / D, RMS_EPS, ALU.mult,
                                  ALU.add).then_inc(ms_ready, 1)
                dve.wait_ge(rms_ready, n + 1)
                dve.reciprocal(rrms[:, t, s:s + 1], rms[:, t, s:s + 1]).then_inc(rrms_ready, 1)

            for t in range(TT):
                over_rms(t, 0)
                dve.wait_ge(rrms_ready, 2 * t + 1)
                dve.scalar_tensor_tensor(out=ks[:, t, :], in0=bank[:, KQV_BANKS[3 * t % 6], :], scalar=rrms[:, t, 0:1],
                                         in1=row("kn"), op0=ALU.mult, op1=ALU.mult).then_inc(kw_ready, 1)
                dve.wait_ge(kw_ready, t + 1)
                dve.tensor_scalar(ks[:, t, :], ks[:, t, :], 0.0, None, ALU.max).then_inc(k_ready, 1)
                over_rms(t, 1)
                if t < 2:
                    low_xT(2 * TT + t + 2, X1_BANKS)
            dve.wait_ge(masks_ready, MASKS)
            for c in range(C):
                dve.wait_ge(kv_psum, c + 1)
                dve.tensor_tensor(kv[:, c, :], bank[:, KV_BANKS[c], 0:VW], kvmask[:], ALU.mult).then_inc(kv_ready, 1)
            for t in range(TT):
                dve.wait_ge(la_psum, t + 1)
                la = bank[:, LA_BANKS[t]:LA_BANKS[t] + 2, 0:2 * VW].rearrange("p b (g w) -> p b g w", g=2)
                dve.tensor_scalar(norm[:, t].rearrange("p (b g) h -> p b g h", b=2), la[:, :, :, P:VW], DEN_EPS, None,
                                  ALU.add).then_inc(norm_ready, 1)
                dve.wait_ge(norm_ready, t + 1)
                dve.reciprocal(rnorm[:, t], norm[:, t]).then_inc(rnorm_ready, 1)
                dve.wait_ge(rnorm_ready, t + 1)
                for b in range(2):
                    ins = dve.tensor_tensor(
                        heads[:, t, b * 2 * P:(b + 1) * 2 * P].rearrange("p (g h e) -> p g h e", g=2, h=HG),
                        la[:, b, :, 0:P].rearrange("p g (h e) -> p g h e", h=HG),
                        rnorm[:, t, 2 * b:2 * b + 2, :].unsqueeze(3).to_broadcast([P, 2, HG, DH]), ALU.mult)
                ins.then_inc(heads_ready, 1)
                if 1 <= t < TT - 1:
                    low_xT(3 * TT + t - 1, HEAD_BANKS)
            for t in range(TT):
                dve.wait_ge(z_psum, t + 1)
                dve.wait_ge(bout_added, t + 1)
                dve.tensor_tensor(xs[:, t, :], xs[:, t, :], bank[:, HEAD_BANKS[t], :], ALU.add).then_inc(x2_ready, 1)
                dve.wait_ge(x2_ready, t + 1)
                ln_stats(2 * TT + t)
                if t < 2:
                    low_xT(3 * TT + 2 + t, HEAD_BANKS)
                else:
                    low_xT(4 * TT + 2 * (t - 2), X2_BANKS)
                ln_scale(2 * TT + t)
                if t == 2:
                    low_xT(4 * TT + 1, X2_BANKS)
            low_xT(4 * TT + 3, X2_BANKS)

            rc = [0]

            def route(ins):
                ins.then_inc(route_step, 1)
                rc[0] += 1
                dve.wait_ge(route_step, rc[0])

            def router():
                dve.wait_ge(scoreT_psum, 1)
                scores = bank[:, 5, 0:TT * E].rearrange("p (t e) -> p t e", t=TT)
                dve.tensor_copy(sig[:], scores).then_inc(route_step, 1)
                rc[0] += 1
                route(dve.tensor_tensor(biased[:], scores, row("rb").unsqueeze(1).to_broadcast([P, TT, E]), ALU.add))
                for t in range(TT):
                    mine = biased[:, t, :].unsqueeze(2).to_broadcast([P, E, E])
                    others = biased[:, t, :].unsqueeze(1).to_broadcast([P, E, E])
                    dve.tensor_tensor(above[:, t], others, mine, ALU.is_gt)
                    ins = dve.tensor_tensor(tied[:, t], others, mine, ALU.is_equal)
                route(ins)
                route(dve.tensor_tensor(tied[:], tied[:], lower[:].unsqueeze(1).to_broadcast([P, TT, E, E]), ALU.mult))
                route(dve.tensor_tensor(above[:], above[:], tied[:], ALU.add))
                route(dve.reduce_sum(rank[:], above[:], AX.X))
                route(dve.scalar_tensor_tensor(out=gate[:], in0=rank[:], scalar=1.5, in1=sig[:], op0=ALU.is_lt, op1=ALU.mult))
                route(dve.reduce_sum(gsum[:], gate[:], AX.X))
                route(dve.tensor_scalar(gsum[:], gsum[:], TOP_EPS, None, ALU.add))
                route(dve.reciprocal(grec[:], gsum[:]))
                dve.tensor_tensor(cw[:], gate[:], grec[:].unsqueeze(2).to_broadcast([P, TT, E]), ALU.mult).then_inc(cw_ready, 1)
                dve.wait_ge(cw_ready, 1)
                route(dve.tensor_tensor(cw_id[:], cw[:, :, 4], cw[:, :, 6], ALU.add))

            def experts(m):
                dve.wait_ge(silu_ready, m + 1)
                dve.wait_ge(u_psum, m + 1)
                wait(dve, hid_ready, m - 1)
                dve.tensor_tensor(hid_full[m % 2][:], act_g[m % 2][:], bank[:, 2 + m % 2, :], ALU.mult).then_inc(hid_full_ready, 1)

            def low_hid(m):
                dve.wait_ge(hidh_ready, m + 1)
                dve.tensor_tensor(hid[m % 3][1][:], hid_full[m % 2][:], hid[m % 3][0][:].bitcast(F32),
                                  ALU.subtract).then_inc(hid_ready, 1)

            terms = [0]
            last_term = [0] * TT

            def add_term(t, in0, scalar):
                wait(dve, xs_added, last_term[t])
                if scalar is None:
                    ins = dve.tensor_tensor(xs[:, t, :], xs[:, t, :], in0, ALU.add)
                else:
                    ins = dve.scalar_tensor_tensor(out=xs[:, t, :], in0=in0, scalar=scalar, in1=xs[:, t, :],
                                                   op0=ALU.mult, op1=ALU.add)
                ins.then_inc(xs_added, 1)
                terms[0] += 1
                last_term[t] = terms[0]

            def add_expert(e):
                for t in range(TT):
                    dve.wait_ge(down_psum, (e * IC + IC - 1) * TT + t + 1)
                    add_term(t, bank[:, 4 + t, :], cw[:, t, e:e + 1])

            convc = [0]

            def conv_chain(ins):
                ins.then_inc(conv_step, 1)
                convc[0] += 1
                dve.wait_ge(conv_step, convc[0])

            dve.wait_ge(pads_ready, 2)
            dve.wait_ge(xf_ready, TT)
            for m in range(M):
                if m >= 4 and m % IC == 0:
                    add_expert(m // IC - 2)
                experts(m)
                if m >= 1:
                    low_hid(m - 1)
                if m == 1:
                    router()
                if 2 <= m < 2 + TT:
                    t = m - 2
                    add_term(t, xn[:, t, :], cw_id[:, t:t + 1])
                    dve.wait_ge(relu_ready, t + 1)
                    add_term(t, relu_x[:, t % 2, :], None)
                if 2 <= m < 2 + C:
                    c = m - 2

                    def tap(j):
                        return cols[:, COLS["conv_w"] + c * TAPS + j:COLS["conv_w"] + c * TAPS + j + 1]

                    conv_chain(dve.tensor_scalar(conv[:, c, :], xf[:, c, 0:T], tap(0), col("conv_b", c), ALU.mult, ALU.add))
                    for j in range(1, TAPS):
                        ins = dve.scalar_tensor_tensor(out=conv[:, c, :], in0=xf[:, c, j:j + T], scalar=tap(j),
                                                       in1=conv[:, c, :], op0=ALU.mult, op1=ALU.add)
                        if j < TAPS - 1:
                            conv_chain(ins)
                    ins.then_inc(conv_ready, 1)
            low_hid(M - 1)
            add_expert(EM - 2)
            for t in range(TT):
                dve.wait_ge(conv_psum, t + 1)
                add_term(t, bank[:, t, :], None)
            for t in range(TT):
                dve.wait_ge(down_psum, (M - 1) * TT + t + 1)
                wait(dve, xs_added, last_term[t])
                dve.scalar_tensor_tensor(out=xs[:, t, :], in0=bank[:, 4 + t, :], scalar=cw[:, t, EM - 1:EM],
                                         in1=xs[:, t, :], op0=ALU.mult, op1=ALU.add).then_inc(out_ready, 1)

        @block.tensor
        def _(pe):
            def transpose_tile(src, t, dst):
                for c in range(C):
                    ins = pe.transpose(bank[:, dst, c * P:(c + 1) * P], src[:, t, c * P:(c + 1) * P], ident[:])
                return ins

            def project(dst, lhs, rhs, starts=True, stops=True, cols=slice(0, 512), rows=slice(0, P)):
                n = len(lhs)
                for c in range(n):
                    (a_h, a_l), (b_h, b_l) = lhs[c], rhs[c]
                    for k, (a, b) in enumerate(((a_h, b_h), (a_h, b_l), (a_l, b_h))):
                        ins = pe.matmul(bank[rows, dst, cols], a, b, start=(starts and c == 0 and k == 0),
                                        stop=(stops and c == n - 1 and k == 2))
                return ins

            def cut(w, c, a, b):
                return w[0][:, c, a:b], w[1][:, c, a:b]

            pe.wait_ge(ident_ready, 2)
            def warm(products):
                for n in range(products):
                    pe.matmul(bank[:, 7, 0:P], ident[:], ident[:], start=True, stop=True)

            warm(WARM)

            def transpose_x(t):
                pe.wait_ge(xn_ready, t + 1)
                transpose_tile(xn, t, XT_BANKS[t]).then_inc(xnT_psum, 1)

            def q_half(h, e):
                pe.wait_ge(xl_ready, 2 * (h + 1))
                pe.wait_ge(wq_ready, e + 1)
                part = slice(h * HALF, (h + 1) * HALF)
                project(Q_BANKS[h][e], [cut(wq, e, c * P, (c + 1) * P) for c in range(C)],
                        [cut(xT, c, part.start, part.stop) for c in range(C)], cols=part).then_inc(q_psum, 1)

            transpose_x(0)
            warm(KEEP_WARM)
            transpose_x(1)
            warm(KEEP_WARM)
            q_half(0, 0)
            transpose_x(2)
            q_half(0, 1)
            transpose_x(3)
            q_half(0, 2)
            q_half(0, 3)
            for e in range(C):
                q_half(1, e)
            pe.wait_ge(wk_ready, 1)
            for h in range(2):
                pe.wait_ge(qTl_ready, (h + 1) * C)
                part = slice(h * HALF, (h + 1) * HALF)
                for c in range(C):
                    project(Q_BANKS[h][c], [cut(wk, e, c * P, (c + 1) * P) for e in range(C)],
                            [cut(qT, e, part.start, part.stop) for e in range(C)], cols=part).then_inc(qk_psum, 1)
            def scores(i, u):
                t, b, m = u % TT, u % 2, (u // TT) % 2
                if isinstance(i, int) and i < 3:
                    pe.wait_ge(qkl_ready, C + 1 + i if i < 2 else 2 * C)
                if t == 0:
                    pe.wait_ge(ctxl_ready, i + 2)
                wait(pe, exp_done, i - 1)
                ins = project(b, [cut(qk, c, t * P, (t + 1) * P) for c in range(C)],
                              [cut(ct[m], c, 0, KB) for c in range(C)])
                ins.then_inc(s_done, 1)
                if isinstance(i, int) and i == 0:
                    pe.wait_ge(qb_step, 2 * C + 2)
                    pe.wait_ge(ones_ready, 1)
                    for n in range(TT):
                        ins = pe.matmul(bank[:, 4, n:n + 1], qb[:, 0, n * P:(n + 1) * P], ones[:], start=True, stop=True)
                    ins.then_inc(keyb_psum, 1)

            def transposes(i, u):
                b = u % 2
                pe.wait_ge(exp_done, i + 1)
                wait(pe, ptl_ready, i - 1)
                for c in range(KC):
                    ins = pe.transpose(bank[:, 2 + b, c * P:(c + 1) * P], probs[b][:, c * P:(c + 1) * P], ident[:])
                ins.then_inc(t_done, 1)

            def weighted_sums(i, u):
                t, b, m = u % TT, u % 2, (u // TT) % 2
                pe.wait_ge(ptl_ready, i + 1)
                if t == 0:
                    pe.wait_ge(ctxl_ready, i + 4)
                wait(pe, acc_done, i - 1)
                ins = project(4 + b, [cut(pt[b], c, 0, P) for c in range(KC)],
                              [cut(cn[m], c, 0, D) for c in range(KC)])
                ins.then_inc(pv_done, 1)

            def step(i, u, last=False):
                if not (isinstance(i, int) and i >= STEPS):
                    scores(i, u)
                if not (isinstance(i, int) and (i < 1 or i > STEPS)):
                    transposes(i - 1, (u - 1) % GROUP)
                if not (isinstance(i, int) and i < 2):
                    weighted_sums(i - 2, (u - 2) % GROUP)

            over_steps(pe, step)

            def transpose_output(t):
                pe.wait_ge(xn_ready, TT + t + 1)
                transpose_tile(acc, t, ON_BANKS[t]).then_inc(xnT_psum, 1)

            def v_half(h, e):
                pe.wait_ge(xl_ready, TT + 2 * (h + 1))
                part = slice(h * HALF, (h + 1) * HALF)
                project(V_BANKS[h][e], [cut(wv, c, e * P, (e + 1) * P) for c in range(C)],
                        [cut(xT, c, part.start, part.stop) for c in range(C)], cols=part).then_inc(v_psum, 1)

            transposes(STEPS - 1, GROUP - 1)
            transpose_output(0)
            weighted_sums(STEPS - 2, GROUP - 2)
            transpose_output(1)
            weighted_sums(STEPS - 1, GROUP - 1)
            transpose_output(2)
            pe.wait_ge(ptl_ready, STEPS)
            v_half(0, 0)
            v_half(0, 1)
            transpose_output(3)
            pe.wait_ge(acc_done, STEPS)
            v_half(0, 2)
            v_half(0, 3)
            for e in range(C):
                v_half(1, e)

            def transpose_x1(t):
                pe.wait_ge(xn_ready, 2 * TT + t + 1)
                transpose_tile(xn, t, X1_BANKS[t]).then_inc(xnT_psum, 1)

            for t in range(TT):
                pe.wait_ge(vTl_ready, (t // 2 + 1) * C)
                if t == TT - 1:
                    transpose_x1(0)
                project(Y_BANKS[t], [cut(vT, e, t * P, (t + 1) * P) for e in range(C)],
                        [cut(wo, e, 0, D) for e in range(C)]).then_inc(y_psum, 1)
            transpose_x1(1)

            def transpose_q(t):
                pe.wait_ge(qs_ready, t + 1)
                wait(pe, qrT_ready, t - 1)
                for c in range(C):
                    ins = pe.transpose(bank[:, QT_BANKS[t % 2], c * P:(c + 1) * P], qs[:, t, c * P:(c + 1) * P], ident[:])
                ins.then_inc(qsT_psum, 1)

            pe.wait_ge(ctxl_ready, (NB + 2) * TT)
            for t in range(TT):
                pe.wait_ge(xl_ready, 2 * TT + t + 1)
                for s, (w, done) in enumerate(((wqkv[1], k2_psum), (wqkv[0], q2_psum), (wqkv[2], v2_psum))):
                    n = 3 * t + s
                    if n < 4:
                        pe.wait_ge(x1_ready, n + 1)
                    elif n < 6:
                        pe.wait_ge(xl_ready, 2 * TT + n - 3)
                    if n >= 6:
                        pe.wait_ge((kw_ready, qs_ready, v_ready)[s], t - 1)
                    project(KQV_BANKS[n % 6], [cut(xT, c, t * P, (t + 1) * P) for c in range(C)],
                            [cut(w, c, 0, D) for c in range(C)]).then_inc(done, 1)
                if t < 2:
                    transpose_x1(t + 2)
                if t >= 1:
                    if t == 1:
                        pe.wait_ge(xl_ready, 3 * TT - 1)
                    if t == 2:
                        pe.wait_ge(xl_ready, 3 * TT)
                    transpose_q(t - 1)
            transpose_q(TT - 1)
            pe.wait_ge(kw_ready, TT)
            pe.wait_ge(v_ready, TT)
            pe.wait_ge(k_ready, TT)
            pe.wait_ge(pads_ready, 1)
            for c in range(C):
                for t in range(TT):
                    ins = pe.matmul(bank[:, KV_BANKS[c], 0:VW], ks[:, t, c * P:(c + 1) * P], vs[:, t, c, :],
                                    start=(t == 0), stop=(t == TT - 1))
                ins.then_inc(kv_psum, 1)
            def linear(t):
                pe.wait_ge(qrT_ready, TT)
                for c in range(C):
                    if t == 0:
                        pe.wait_ge(kv_ready, c + 1)
                    ins = pe.matmul(bank[:, LA_BANKS[t] + c // 2, c % 2 * VW:(c % 2 + 1) * VW],
                                    qrT[:, c, t * P:(t + 1) * P], kv[:, c, :], start=True, stop=True)
                ins.then_inc(la_psum, 1)

            for t in range(TT - 1):
                linear(t)

            def transpose_heads(t):
                pe.wait_ge(heads_ready, t + 1)
                transpose_tile(heads, t, HEAD_BANKS[t]).then_inc(xnT_psum, 1)

            def transpose_x2(t):
                pe.wait_ge(xn_ready, 3 * TT + t + 1)
                transpose_tile(xn, t, X2_BANKS[t]).then_inc(xnT_psum, 1)

            transpose_heads(0)
            linear(TT - 1)
            transpose_heads(1)
            for t in range(TT):
                pe.wait_ge(xl_ready, 3 * TT + t + 1)
                if t == TT - 1:
                    transpose_x2(0)
                    transpose_x2(1)
                project(HEAD_BANKS[t], [cut(xT, c, t * P, (t + 1) * P) for c in range(C)],
                        [cut(wout, c, 0, D) for c in range(C)]).then_inc(z_psum, 1)
                if t < 2:
                    transpose_heads(t + 2)

            def route():
                pe.wait_ge(xf_ready, 1)
                pe.wait_ge(xl_ready, 5 * TT)
                pe.wait_ge(wr_ready, 1)
                project(4, [cut(wr, c, 0, E) for c in range(C)], [cut(xT, c, 0, T) for c in range(C)],
                        rows=slice(0, E)).then_inc(route_psum, 1)

            def expert(kind, e, chunks):
                return [w[:].rearrange("p (c n) -> p c n", c=chunks) for w in piece[order[kind, e]]]

            def gates(m, part=slice(0, T)):
                e, i = m // IC, m % IC
                pe.wait_ge(xl_ready, 4 * TT + part.stop // P)
                pe.wait_ge(piece_ready, order["g", e] + 1)
                wait(pe, silu_ready, m - 1)
                ins = project(m % 2, [cut(expert("g", e, C), c, i * P, (i + 1) * P) for c in range(C)],
                              [cut(xT, c, part.start, part.stop) for c in range(C)], cols=part)
                if part.stop == T:
                    ins.then_inc(g_psum, 1)

            def values(m, part=slice(0, T)):
                e, i = m // IC, m % IC
                pe.wait_ge(piece_ready, order["u", e] + 1)
                wait(pe, hid_full_ready, m - 1)
                ins = project(2 + m % 2, [cut(expert("u", e, C), c, i * P, (i + 1) * P) for c in range(C)],
                              [cut(xT, c, part.start, part.stop) for c in range(C)], cols=part)
                if part.stop == T:
                    ins.then_inc(u_psum, 1)

            def down(m):
                e, i = m // IC, m % IC
                pe.wait_ge(piece_ready, order["d", e] + 1)
                pe.wait_ge(hid_ready, m + 1)
                if m == 0:
                    pe.wait_ge(xf_ready, TT)
                    pe.wait_ge(route_step, 2)
                for t in range(TT):
                    if e > 0 and i == 0:
                        pe.wait_ge(xs_added, terms_with(e - 1, t))
                    project(4 + t, [tuple(h[:, t * P:(t + 1) * P] for h in hid[m % 3])],
                                  [cut(expert("d", e, IC), i, 0, D)], starts=(i == 0),
                            stops=(i == IC - 1)).then_inc(down_psum, 1)

            first, second = slice(0, HALF), slice(HALF, T)
            transpose_x2(2)
            gates(0, first)
            values(0, first)
            pe.wait_ge(x2_ready, TT)
            gates(1, first)
            transpose_x2(3)
            values(1, first)
            for m in range(2):
                gates(m, second)
                values(m, second)
            route()
            for m in range(2, M):
                gates(m)
                if m == 2:
                    pe.wait_ge(sig_ready, 1)
                    pe.wait_ge(xf_ready, 2)
                    for t in range(TT):
                        ins = pe.transpose(bank[:, 5, t * E:(t + 1) * E], score_rows[:, t * P:(t + 1) * P], ident[0:E, 0:E])
                    ins.then_inc(scoreT_psum, 1)
                values(m)
                down(m - 2)
            pe.wait_ge(conv_ready, C)
            pe.wait_ge(silu_ready, M)
            pe.wait_ge(hid_full_ready, M)
            for t in range(TT):
                for c in range(C):
                    ins = pe.transpose(bank[:, t, c * P:(c + 1) * P], conv[:, c, t * P:(t + 1) * P], ident[:])
                ins.then_inc(conv_psum, 1)
            down(M - 2)
            down(M - 1)


def kernel(x, ctx_1024, L0_xattn_Wq, L0_xattn_bq, L0_xattn_Wk, L0_xattn_bk, L0_xattn_Wv, L0_xattn_bv, L0_xattn_Wo,
           L0_xattn_bo, L0_attn_W_qkv, L0_attn_qn_w, L0_attn_kn_w, L0_attn_W_out, L0_attn_b_out, L0_ffn_Wr,
           L0_ffn_router_bias, L0_ffn_Wg, L0_ffn_Wu, L0_ffn_Wd, L0_ffn_conv_w, L0_ffn_conv_b):
    import numpy as np
    import concourse.bacc as bacc
    from concourse.bass_utils import run_bass_kernel_spmd

    def on_partitions(w):
        w = np.asarray(w)
        return np.ascontiguousarray(w.reshape(-1, P, w.shape[-1]).transpose(1, 0, 2))

    def column(v):
        return np.asarray(v).reshape(-1, P).T

    ctx = np.asarray(ctx_1024)[0].reshape(NB, KC, P, C, P)
    wqkv = np.asarray(L0_attn_W_qkv)
    matrices = {"g": L0_ffn_Wg, "u": L0_ffn_Wu, "d": L0_ffn_Wd}
    arrays = {
        "x": np.ascontiguousarray(np.asarray(x)[0].reshape(TT, P, D)),
        "ctx_t": np.ascontiguousarray(ctx.transpose(0, 4, 3, 1, 2).reshape(NB, P, C, KB)),
        "ctx_n": np.ascontiguousarray(ctx.transpose(0, 2, 1, 3, 4).reshape(NB, P, KC, D)),
        "wq_t": np.ascontiguousarray(np.asarray(L0_xattn_Wq).reshape(C, P, C, P).transpose(0, 3, 2, 1).reshape(C, P, D)),
        "wk_in": on_partitions(L0_xattn_Wk),
        "wv_t": on_partitions(np.asarray(L0_xattn_Wv).T),
        "wo_t": on_partitions(np.asarray(L0_xattn_Wo).T),
        "wqkv_in": np.stack([on_partitions(wqkv[:, s * D:(s + 1) * D]) for s in range(3)]),
        "wout_in": on_partitions(L0_attn_W_out),
        "pieces": np.stack([on_partitions(np.asarray(matrices[kind])[e]).reshape(P, PIECE) for kind, e in PIECES]),
        "cols_in": np.ascontiguousarray(np.concatenate(
            [column(L0_xattn_bq), column(L0_xattn_bk), column(L0_xattn_bv), column(L0_attn_qn_w),
             column(L0_ffn_conv_b),
             np.asarray(L0_ffn_conv_w).reshape(TAPS, C, P).transpose(2, 1, 0).reshape(P, C * TAPS),
             on_partitions(L0_ffn_Wr).reshape(P, C * E)], axis=1)),
        "rows_in": np.concatenate([np.asarray(v).reshape(-1) for v in
                                   (L0_xattn_bo, L0_attn_kn_w, L0_attn_b_out, L0_ffn_router_bias)]),
    }
    nc = bacc.Bacc("TRN2", target_bir_lowering=False, num_devices=1)
    args = {name: nc.dram_tensor(name, a.shape, mybir.dt.from_np(a.dtype), kind="ExternalInput").ap()
            for name, a in arrays.items()}
    out = nc.dram_tensor("out", (TT, P, D), F32, kind="ExternalOutput").ap()
    perceiver_block(nc, **args, out=out)
    result = run_bass_kernel_spmd(nc, [arrays], core_ids=[0])
    return result.results[0]["out"].reshape(1, T, D)
```
